# Optimizing a Trainium2 kernel written in Bass

```python
import numpy as np
import jax
import jax.numpy as jnp

def _softmax(x, axis=-1):
    return jax.nn.softmax(x, axis=axis)

def _gelu(x):
    return jax.nn.gelu(x, approximate=True)

def _silu(x):
    return jax.nn.silu(x)

def _sigmoid(x):
    return jax.nn.sigmoid(x)

def _layernorm(x, axis=-1, eps=1e-05):
    m = jnp.mean(x, axis=axis, keepdims=True)
    v = jnp.var(x, axis=axis, keepdims=True)
    return (x - m) / jnp.sqrt(v + eps)

def _scatter_add(tgt, idx, src, axis=0):
    return tgt.at[idx].add(src)

def _segment_sum(src, seg, n):
    return jax.ops.segment_sum(src, seg, n)
kernel_name = 'mk_audio_tower_d1_tok_aud1d768_r4_b289b8'

def setup_inputs(seed: int=0):
    np.random.seed(seed)
    _w = jnp.asarray

    def _rec_inputs():
        import jax
        import jax.numpy as jnp
        _rk = jax.random.key(seed)
        x = -0.000869125 + 1.00042 * jax.random.normal(jax.random.fold_in(_rk, 1), (64, 4000), jnp.float32)
        return x
    x = _rec_inputs()

    def _L0_tok_setup():
        import jax, jax.numpy as jnp
        import numpy as np
        CONVS = [(128, 10, 5)] + [(128, 3, 2)] * 4 + [(128, 2, 2)] * 2

        def _fp32_layernorm(x, g, b, eps=1e-05):
            xf = x.astype(jnp.float32)
            mu = xf.mean(-1, keepdims=True)
            var = xf.var(-1, keepdims=True)
            y = (xf - mu) * jax.lax.rsqrt(var + eps) * g.astype(jnp.float32) + b.astype(jnp.float32)
            return y.astype(x.dtype)

        def _conv1d(x, w, stride):
            return jax.lax.conv_general_dilated(x, w, (stride,), 'VALID', dimension_numbers=('NCH', 'OIH', 'NCH'))
        key = jax.random.key(seed)
        keys = jax.random.split(key, 16)
        inp = {'x': jax.random.normal(keys[0], (8, 40000), jnp.float32)}
        in_d = 1
        for i, (dim, k, s) in enumerate(CONVS):
            fan_in = in_d * k
            inp[f'conv_w{i}'] = jax.random.normal(keys[1 + i], (dim, in_d, k), jnp.float32) * np.float32(np.sqrt(2.0 / fan_in))
            inp[f'ln_g{i}'] = jnp.ones((dim,), jnp.float32)
            inp[f'ln_b{i}'] = jnp.zeros((dim,), jnp.float32)
            in_d = dim
        inp['fln_g'] = jnp.ones((128,), jnp.float32)
        inp['fln_b'] = jnp.zeros((128,), jnp.float32)
        inp['proj_w'] = jax.random.normal(keys[9], (128, 192), jnp.float32) * np.float32(0.02)
        inp['proj_b'] = jnp.zeros((192,), jnp.float32)
        return inp
    _L0_tok_all = _L0_tok_setup()
    _L0_tok_in = {k: v for k, v in _L0_tok_all.items() if k in ('conv_w0', 'ln_g0', 'ln_b0', 'conv_w1', 'ln_g1', 'ln_b1', 'conv_w2', 'ln_g2', 'ln_b2', 'conv_w3', 'ln_g3', 'ln_b3', 'conv_w4', 'ln_g4', 'ln_b4', 'conv_w5', 'ln_g5', 'ln_b5', 'conv_w6', 'ln_g6', 'ln_b6', 'fln_g', 'fln_b', 'proj_w', 'proj_b')}
    del _L0_tok_all

    def _L0_attn_setup():
        import jax, jax.numpy as jnp
        import numpy as np
        B, N, C = (4, 256, 192)
        HEAD_DIM = 32
        NUM_HEADS = C // HEAD_DIM
        SCALE = HEAD_DIM ** (-0.5)
        key = jax.random.key(seed)
        k1, k2, k3 = jax.random.split(key, 3)
        x = jax.random.normal(k1, (B, N, C), dtype=jnp.float32)
        w_qkv = jax.random.normal(k2, (C, 3 * NUM_HEADS * HEAD_DIM), dtype=jnp.float32) * C ** (-0.5)
        w_proj = jax.random.normal(k3, (NUM_HEADS * HEAD_DIM, C), dtype=jnp.float32) * C ** (-0.5)
        return {'x': x, 'w_qkv': w_qkv, 'w_proj': w_proj}
    _L0_attn_all = _L0_attn_setup()
    _L0_attn_in = {k: v for k, v in _L0_attn_all.items() if k in ('w_qkv', 'w_proj')}
    del _L0_attn_all

    def _L0_ffn_setup():
        import jax, jax.numpy as jnp
        import numpy as np
        D_MODEL = 192
        D_FF = 768
        N_EXPERTS = 9
        key = jax.random.key(seed)
        ks = jax.random.split(key, 7)
        scale = 0.02
        return {'x': jax.random.normal(ks[0], (2, 256, D_MODEL), jnp.float32), 'Ws': jax.random.normal(ks[1], (D_MODEL, N_EXPERTS), jnp.float32) * scale, 'bs': jnp.zeros((N_EXPERTS,), jnp.float32), 'W1': jax.random.normal(ks[2], (N_EXPERTS, D_MODEL, D_FF), jnp.float32) * scale, 'b1': jnp.zeros((N_EXPERTS, D_FF), jnp.float32), 'W2': jax.random.normal(ks[3], (N_EXPERTS, D_FF, D_MODEL), jnp.float32) * scale, 'b2': jnp.zeros((N_EXPERTS, D_MODEL), jnp.float32)}
    _L0_ffn_all = _L0_ffn_setup()
    _L0_ffn_in = {k: v for k, v in _L0_ffn_all.items() if k in ('Ws', 'bs', 'W1', 'b1', 'W2', 'b2')}
    del _L0_ffn_all
    return {'x': x, 'L0_tok_conv_w0': _L0_tok_in['conv_w0'], 'L0_tok_ln_g0': _L0_tok_in['ln_g0'], 'L0_tok_ln_b0': _L0_tok_in['ln_b0'], 'L0_tok_conv_w1': _L0_tok_in['conv_w1'], 'L0_tok_ln_g1': _L0_tok_in['ln_g1'], 'L0_tok_ln_b1': _L0_tok_in['ln_b1'], 'L0_tok_conv_w2': _L0_tok_in['conv_w2'], 'L0_tok_ln_g2': _L0_tok_in['ln_g2'], 'L0_tok_ln_b2': _L0_tok_in['ln_b2'], 'L0_tok_conv_w3': _L0_tok_in['conv_w3'], 'L0_tok_ln_g3': _L0_tok_in['ln_g3'], 'L0_tok_ln_b3': _L0_tok_in['ln_b3'], 'L0_tok_conv_w4': _L0_tok_in['conv_w4'], 'L0_tok_ln_g4': _L0_tok_in['ln_g4'], 'L0_tok_ln_b4': _L0_tok_in['ln_b4'], 'L0_tok_conv_w5': _L0_tok_in['conv_w5'], 'L0_tok_ln_g5': _L0_tok_in['ln_g5'], 'L0_tok_ln_b5': _L0_tok_in['ln_b5'], 'L0_tok_conv_w6': _L0_tok_in['conv_w6'], 'L0_tok_ln_g6': _L0_tok_in['ln_g6'], 'L0_tok_ln_b6': _L0_tok_in['ln_b6'], 'L0_tok_fln_g': _L0_tok_in['fln_g'], 'L0_tok_fln_b': _L0_tok_in['fln_b'], 'L0_tok_proj_w': _L0_tok_in['proj_w'], 'L0_tok_proj_b': _L0_tok_in['proj_b'], 'L0_attn_w_qkv': _L0_attn_in['w_qkv'], 'L0_attn_w_proj': _L0_attn_in['w_proj'], 'L0_ffn_Ws': _L0_ffn_in['Ws'], 'L0_ffn_bs': _L0_ffn_in['bs'], 'L0_ffn_W1': _L0_ffn_in['W1'], 'L0_ffn_b1': _L0_ffn_in['b1'], 'L0_ffn_W2': _L0_ffn_in['W2'], 'L0_ffn_b2': _L0_ffn_in['b2']}

def reference(x, L0_tok_conv_w0, L0_tok_ln_g0, L0_tok_ln_b0, L0_tok_conv_w1, L0_tok_ln_g1, L0_tok_ln_b1, L0_tok_conv_w2, L0_tok_ln_g2, L0_tok_ln_b2, L0_tok_conv_w3, L0_tok_ln_g3, L0_tok_ln_b3, L0_tok_conv_w4, L0_tok_ln_g4, L0_tok_ln_b4, L0_tok_conv_w5, L0_tok_ln_g5, L0_tok_ln_b5, L0_tok_conv_w6, L0_tok_ln_g6, L0_tok_ln_b6, L0_tok_fln_g, L0_tok_fln_b, L0_tok_proj_w, L0_tok_proj_b, L0_attn_w_qkv, L0_attn_w_proj, L0_ffn_Ws, L0_ffn_bs, L0_ffn_W1, L0_ffn_b1, L0_ffn_W2, L0_ffn_b2):
    import jax
    import jax.numpy as jnp

    def _L0_tok_ref(x, conv_w0, ln_g0, ln_b0, conv_w1, ln_g1, ln_b1, conv_w2, ln_g2, ln_b2, conv_w3, ln_g3, ln_b3, conv_w4, ln_g4, ln_b4, conv_w5, ln_g5, ln_b5, conv_w6, ln_g6, ln_b6, fln_g, fln_b, proj_w, proj_b):
        import jax, jax.numpy as jnp
        import numpy as np
        CONVS = [(128, 10, 5)] + [(128, 3, 2)] * 4 + [(128, 2, 2)] * 2

        def _fp32_layernorm(x, g, b, eps=1e-05):
            xf = x.astype(jnp.float32)
            mu = xf.mean(-1, keepdims=True)
            var = xf.var(-1, keepdims=True)
            y = (xf - mu) * jax.lax.rsqrt(var + eps) * g.astype(jnp.float32) + b.astype(jnp.float32)
            return y.astype(x.dtype)

        def _conv1d(x, w, stride):
            return jax.lax.conv_general_dilated(x, w, (stride,), 'VALID', dimension_numbers=('NCH', 'OIH', 'NCH'))
        conv_ws = [conv_w0, conv_w1, conv_w2, conv_w3, conv_w4, conv_w5, conv_w6]
        ln_gs = [ln_g0, ln_g1, ln_g2, ln_g3, ln_g4, ln_g5, ln_g6]
        ln_bs = [ln_b0, ln_b1, ln_b2, ln_b3, ln_b4, ln_b5, ln_b6]
        strides = [s for _, _, s in CONVS]
        h = x[:, None, :]
        for w, g, b, s in zip(conv_ws, ln_gs, ln_bs, strides):
            h = _conv1d(h, w, s)
            h = jnp.swapaxes(h, -2, -1)
            h = _fp32_layernorm(h, g, b)
            h = jnp.swapaxes(h, -2, -1)
            h = jax.nn.gelu(h, approximate=False)
        h = jnp.swapaxes(h, 1, 2)
        norm_h = _fp32_layernorm(h, fln_g, fln_b)
        out = norm_h @ proj_w + proj_b
        return out

    def _L0_attn_ref(x, w_qkv, w_proj):
        import jax, jax.numpy as jnp
        import numpy as np
        B, N, C = (4, 256, 192)
        HEAD_DIM = 32
        NUM_HEADS = C // HEAD_DIM
        SCALE = HEAD_DIM ** (-0.5)
        b, n, c = x.shape
        qkv = (x @ w_qkv).reshape(b, n, 3, NUM_HEADS, HEAD_DIM).transpose(2, 0, 3, 1, 4)
        q, k, v = (qkv[0], qkv[1], qkv[2])
        attn = jnp.einsum('bhqd,bhkd->bhqk', q, k) * SCALE
        attn = jax.nn.softmax(attn, axis=-1)
        out = jnp.einsum('bhqk,bhkd->bhqd', attn, v)
        out = out.transpose(0, 2, 1, 3).reshape(b, n, c)
        return out @ w_proj

    def _L0_ffn_ref(x, Ws, bs, W1, b1, W2, b2):
        import jax, jax.numpy as jnp
        import numpy as np
        D_MODEL = 192
        D_FF = 768
        N_EXPERTS = 9
        B, S, d = x.shape
        xt = x.reshape(-1, d)
        route_prob = jax.nn.softmax(xt @ Ws + bs, axis=-1)
        p = jnp.max(route_prob, axis=-1)
        routes = jnp.argmax(route_prob, axis=-1)
        h = jax.nn.gelu(jnp.einsum('td,edf->tef', xt, W1) + b1, approximate=False)
        out = jnp.einsum('tef,efd->ted', h, W2) + b2
        common = out[:, 0, :]
        sel = jnp.take_along_axis(out, routes[:, None, None], axis=1)[:, 0, :]
        scaling = (p / jax.lax.stop_gradient(p))[:, None]
        pe = p[:, None]
        final = jnp.where((routes == 0)[:, None], common * scaling, pe * sel + (1.0 - pe) * common)
        return final.reshape(B, S, d)
    h = _L0_tok_ref(x, L0_tok_conv_w0, L0_tok_ln_g0, L0_tok_ln_b0, L0_tok_conv_w1, L0_tok_ln_g1, L0_tok_ln_b1, L0_tok_conv_w2, L0_tok_ln_g2, L0_tok_ln_b2, L0_tok_conv_w3, L0_tok_ln_g3, L0_tok_ln_b3, L0_tok_conv_w4, L0_tok_ln_g4, L0_tok_ln_b4, L0_tok_conv_w5, L0_tok_ln_g5, L0_tok_ln_b5, L0_tok_conv_w6, L0_tok_ln_g6, L0_tok_ln_b6, L0_tok_fln_g, L0_tok_fln_b, L0_tok_proj_w, L0_tok_proj_b)
    h = h + _L0_attn_ref(_layernorm(h, axis=-1), L0_attn_w_qkv, L0_attn_w_proj)
    h = h + _L0_ffn_ref(_layernorm(h, axis=-1), L0_ffn_Ws, L0_ffn_bs, L0_ffn_W1, L0_ffn_b1, L0_ffn_W2, L0_ffn_b2)
    return h

_drawn_inputs = setup_inputs


def setup_inputs(seed=0):
    import zlib

    import numpy as np

    out = dict(_drawn_inputs(seed))
    spreads = {'L0_tok_ln_g0': (1.0, 0.2),
     'L0_tok_ln_b0': (0.0, 0.1),
     'L0_tok_ln_g1': (1.0, 0.2),
     'L0_tok_ln_b1': (0.0, 0.1),
     'L0_tok_ln_g2': (1.0, 0.2),
     'L0_tok_ln_b2': (0.0, 0.1),
     'L0_tok_ln_g3': (1.0, 0.2),
     'L0_tok_ln_b3': (0.0, 0.1),
     'L0_tok_ln_g4': (1.0, 0.2),
     'L0_tok_ln_b4': (0.0, 0.1),
     'L0_tok_ln_g5': (1.0, 0.2),
     'L0_tok_ln_b5': (0.0, 0.1),
     'L0_tok_ln_g6': (1.0, 0.2),
     'L0_tok_ln_b6': (0.0, 0.1),
     'L0_tok_fln_g': (1.0, 0.2),
     'L0_tok_fln_b': (0.0, 0.1),
     'L0_tok_proj_b': (0.0, 0.1),
     'L0_ffn_bs': (0.0, 0.355),
     'L0_ffn_b1': (0.0, 0.1),
     'L0_ffn_b2': (0.0, 0.1)}
    factors = {}
    for name, (base, spread) in spreads.items():
        noise = np.random.default_rng([zlib.crc32(name.encode()), seed]).standard_normal(out[name].shape)
        drawn = base * np.exp(spread * noise) if base else spread * noise
        out[name] = jnp.asarray(drawn.astype(out[name].dtype))
    for name, factor in factors.items():
        out[name] = (out[name] * factor).astype(out[name].dtype)
    return out
```

```python
import numpy as np
import concourse.bass as bass
from concourse import mybir
from contextlib import ExitStack

F32 = mybir.dt.float32
ALU = mybir.AluOpType
ACT = mybir.ActivationFunctionType
X = mybir.AxisListType.X

P = 128
BATCH, SAMPLES = 64, 4000
C = 128
CONVS = [(10, 5), (3, 2), (3, 2), (3, 2), (3, 2), (2, 2), (2, 2)]
NT = 8
BT = BATCH // NT
D = 192
D1 = D - P
TOK = 12
M = BT * TOK
NH, HD = 6, 32
DFF, NE = 768, 9
NF = DFF // P
EPS = 1e-5
SCALE = float(HD) ** -0.5

PITCH = [800, 400, 200, 100, 50, 25, 12]
FLAT = [BT * p for p in PITCH]
LAST5 = 24

def cut(layer, per, counts, start=0):
    out = []
    for c in counts:
        out.append((layer, start, per, c))
        start += per * c
    return out

G0 = cut(0, 128, [3] * 14 + [4] * 2)
G1 = cut(1, 128, [4] * 4 + [3] * 3)
G2 = cut(2, 128, [4] * 2) + cut(2, 96, [3] * 2, 1024)
G3 = cut(3, 128, [4]) + cut(3, 96, [3], 512)
G4 = cut(4, 100, [4])
G5 = cut(5, 100, [2])
G6 = cut(6, M, [1])
SHALLOW = G0 + G1
DEEP = G2 + G3 + G4 + G5 + G6
LAG = 3
YBUF, SQBUF, XHBUF, TRBUF, XR = 4, 2, 2, 2, 4


def reads(group):
    layer, start, per, count = group
    if layer == 0:
        return 0, 0
    k, s = CONVS[layer]
    if layer == 6:
        return 0, FLAT[5]
    return s * start, min(s * (start + per * count - 1) + k, FLAT[layer - 1])


def feeds(a, b):
    lo, hi = reads(b)
    return a[0] == b[0] - 1 and a[1] < hi and a[1] + a[2] * a[3] > lo


def order():
    todo = [[(1, g) for g in DEEP], [(0, g) for g in G0], [(0, g) for g in G1]]
    seq = []

    def ready(item):
        at = len(seq)
        for k, s in enumerate(seq):
            if s[0] == item[0] and feeds(s[1], item[1]) and at - k < LAG + 2:
                return False
        if item[0] == 1 and item[1][0] == 2 and at < LAG + 2:
            return False
        return True

    while any(todo):
        deep, first, second = todo
        if deep and ready(deep[0]):
            seq.append(deep.pop(0))
        elif first:
            seq.append(first.pop(0))
        elif second and ready(second[0]):
            seq.append(second.pop(0))
        else:
            raise ValueError(f"no group is ready: {seq} {todo}")
    return seq


BODY = order()
for w, (d, g) in enumerate(BODY):
    if d == 0 and g[0] == 1:
        assert all(r <= w + LAG for r, s in enumerate(BODY) if s[0] == 1 and feeds(g, s[1])), (w, g)
NB = len(BODY)
assert NB % 4 == 0, NB
HEAD = [g for g in BODY if g[0] == 0]
NHD = len(HEAD)
TAIL = [g for g in BODY if g[0] == 1]


def spread(groups):
    slots = [(k - LAG, BODY[k - LAG][1]) for k in range(LAG)]
    for k, (_, g) in enumerate(groups):
        while any(s and feeds(s[1], g) for s in slots[-LAG:]):
            slots.append(None)
        slots.append((k, g))
    return slots + [None] * LAG


ENDING = spread(TAIL)
NG = NHD + (NT - 1) * NB + len(TAIL)
W_TAPS = [(l, t) for l in range(1, 7) for t in range(CONVS[l][0])]
TAP0 = {l: W_TAPS.index((l, 0)) for l in range(1, 7)}
NTAP = len(W_TAPS)


def audio_tower(nc, a, out):
    ctx = ExitStack()
    with ctx:
        def sb(name, shape, dt=F32):
            return ctx.enter_context(nc.sbuf_tensor(name, shape, dt))

        def sem(name):
            return ctx.enter_context(nc.semaphore(name))

        h = [sb(f"h{l}", [P, FLAT[l] + (l < 4) if l < 5 else BT * LAST5]) for l in range(6)]
        h6 = sb("h6", [P, NT * M])
        xr = sb("xr", [10, XR, 2560])
        w0t = sb("w0t", [10, C])
        wt = sb("wt", [P, NTAP, C])
        wraw = sb("wraw", [P, NTAP, C])
        w0raw = sb("w0raw", [P, 10])
        lnraw = sb("lnraw", [16, C])
        lncol = sb("lncol", [P, 16])
        wmean = sb("wmean", [P, 4])
        wscaled = sb("wscaled", [P, 4])
        ident = sb("ident", [P, P])
        mask = sb("mask", [M, M])
        neghalf = sb("neghalf", [P, 4])
        eps = sb("eps", [P, 1])
        ceps = sb("ceps", [P, 4])
        sq = sb("sq", [P, SQBUF, 512])
        xh = sb("xh", [P, XHBUF, 512])
        ssum = sb("ssum", [P, YBUF, 4])
        varv = sb("varv", [P, YBUF, 4])
        rstd = sb("rstd", [P, YBUF, 4])

        projw = sb("projw", [P, D])
        projb = sb("projb", [1, D])
        wqkv = sb("wqkv", [P, 2, 3 * D])
        wprj = sb("wprj", [P, 2, D])
        wsr = sb("wsr", [P, 2, NE])
        ones = sb("ones", [1, P])
        iota = sb("iota", [M, NE])
        W1s = sb("W1s", [P, 2, DFF])
        W2s = sb("W2s", [P, 2, NF, D])
        W1b = sb("W1b", [D1 + 1, 2, DFF])
        b2s = sb("b2s", [1, NE * D])
        xt = sb("xt", [P, NT * M])
        xtb = sb("xtb", [D1 + 1, NT * M])
        acc = sb("acc", [M, NT, D])
        coef = sb("coef", [M, NE, NT])

        stats = sb("stats", [M, 6])
        mv = sb("mv", [M, 2])
        veps = sb("veps", [M, 1])
        rs = sb("rs", [M, 1])
        xn = sb("xn", [M, D])
        act = sb("act", [P, 2, M])
        x1 = sb("x1", [M, D])
        qm = sb("qm", [P, NH, M])
        kT = sb("kT", [P, 2, M])
        vv = sb("vv", [M, D])
        t1 = sb("t1", [M, NH, M])
        mx = sb("mx", [M, NH])
        den = sb("den", [M, NH])
        rden = sb("rden", [M, NH])
        pT = sb("pT", [M, NH, M])
        oo = sb("oo", [M, D])
        lg = sb("lg", [M, NE])
        lgt = sb("lgt", [M, NE])
        s1 = sb("s1", [M, 8])
        hs = sb("hs", [M, 2, DFF])
        hT = sb("hT", [P, 2, 2, 3 * M])

        ps = ctx.enter_context(nc.psum_tensor("ps", [P, 8, 512], F32))
        y = [ps[:, i, :] for i in range(4)]
        tr = [ps[:, 4 + i, :] for i in range(2)]
        pa, pb = ps[:, 6, :], ps[:, 7, :]

        s_w = sem("s_w")
        s_ln = sem("s_ln")
        s_ident = sem("s_ident")
        s_const = sem("s_const")
        s_w0raw = sem("s_w0raw")
        s_pad = sem("s_pad")
        s_wtr = sem("s_wtr")
        s_wmean = sem("s_wmean")
        s_wscaled = sem("s_wscaled")
        s_shares = sem("s_shares")
        s_wt = sem("s_wt")
        s_lnc = sem("s_lnc")
        s_x = [sem(f"s_x{i}") for i in range(XR)]
        conv_done = sem("conv_done")
        sq_done = sem("sq_done")
        ssum_done = sem("ssum_done")
        varv_done = sem("varv_done")
        rstd_done = sem("rstd_done")
        xh_done = sem("xh_done")
        tr_done = sem("tr_done")
        act_done = sem("act_done")
        s_tw = sem("s_tw")
        t = {k: sem("t_" + k) for k in
             "h6c h6r st1 mv1 ve1 rs1 xh1 xhT a1 pj x1 st2 mv2 ve2 rs2 xn2 xn2T a2 qkv qk sc msk mx sub ex den rden pT pTc "
             "pv oo ooT a3 at x2 st3 mv3 ve3 rs3 xn3 xn3T a4 lo lg mxl subl exl suml pmax cand first hot coef fin".split()}
        f_h = sem("f_h")
        f_g = sem("f_g")
        f_t = sem("f_t")
        f_c = sem("f_c")
        f_o = sem("f_o")
        f_acc = sem("f_acc")
        f_w = [sem("f_w0"), sem("f_w1")]
        s_out = sem("s_out")

        block = ctx.enter_context(nc.Block())

        def shifted(off, cols):
            return bass.AP(a["x"].tensor, off, [[1, 10], [1, cols]])

        @block.sync
        def _(sp):
            for l in range(1, 7):
                k = CONVS[l][0]
                sp.dma_start(wraw[:, TAP0[l]:TAP0[l] + k, :].rearrange("p t c -> p (t c)"),
                             a[f"L0_tok_conv_w{l}"].rearrange("o i k -> o (i k)")).then_inc(s_w, 16)
            sp.dma_start(w0raw[:, :], a["L0_tok_conv_w0"].rearrange("o i k -> o (i k)")).then_inc(s_w0raw, 16)
            for l in range(7):
                sp.dma_start(lnraw[l:l + 1, :], a[f"L0_tok_ln_g{l}"].rearrange("(a c) -> a c", a=1)).then_inc(s_ln, 16)
                sp.dma_start(lnraw[8 + l:9 + l, :], a[f"L0_tok_ln_b{l}"].rearrange("(a c) -> a c", a=1)).then_inc(s_ln, 16)
            sp.dma_start(lnraw[7:8, :], a["L0_tok_fln_g"].rearrange("(a c) -> a c", a=1)).then_inc(s_ln, 16)
            sp.dma_start(lnraw[15:16, :], a["L0_tok_fln_b"].rearrange("(a c) -> a c", a=1)).then_inc(s_ln, 16)

            def load_x(i, g, read_by, short=False):
                _, start, per, count = G0[g]
                cols = 5 * per * count - (9 if short else 0)
                if read_by is not None:
                    sp.wait_ge(conv_done, read_by + 1)
                sp.dma_start(xr[:, g % XR, 0:cols], shifted(i * (BT * SAMPLES) + 5 * start, cols))\
                    .then_inc(s_x[g % XR], 16)

            head_at = [HEAD.index((0, g)) for g in G0]
            body_at = [BODY.index((0, g)) for g in G0]
            for g in range(len(G0)):
                load_x(0, g, head_at[g - XR] if g >= XR else None)
            for g in range(XR):
                load_x(1, g, head_at[g - XR])

            def later(i, last):
                step = NHD + (i - 1) * NB
                for g in range(XR, len(G0)):
                    load_x(i, g, step + body_at[g - XR], short=last and g == len(G0) - 1)
                if not last:
                    for g in range(XR):
                        load_x(i + 1, g, step + body_at[g - XR])

            with sp.Fori(1, NT - 1) as i:
                later(i, False)
            later(NT - 1, True)

            def load_expert(e):
                sp.dma_start(W1s[:, e % 2, :], a["L0_ffn_W1"][e, 0:P, :]).then_inc(f_w[e % 2], 16)
                sp.dma_start(W1b[0:D1, e % 2, :], a["L0_ffn_W1"][e, P:D, :]).then_inc(f_w[e % 2], 16)
                sp.dma_start(W1b[D1:D1 + 1, e % 2, :], a["L0_ffn_b1"][e:e + 1, :]).then_inc(f_w[e % 2], 16)
                sp.dma_start(W2s[:, e % 2, :, :], a["L0_ffn_W2"][e].rearrange("(f p) d -> p f d", p=P)).then_inc(f_w[e % 2], 16)

            for e in range(NE):
                if e >= 2:
                    sp.wait_ge(f_o, (e - 1) * NT)
                load_expert(e)
            sp.wait_ge(f_acc, NE * NT)
            sp.dma_start(out.rearrange("(i b) t d -> (b t) i d", i=NT), acc[:, :, :]).then_inc(s_out, 16)
            sp.wait_ge(s_out, 16)

        @block.gpsimd
        def _(gp):
            gp.memset(ident[:, :], 0.0).then_inc(s_ident, 1)
            gp.wait_ge(s_ident, 1)
            gp.affine_select(out=ident[:, :], in_=ident[:, :], compare_op=ALU.not_equal, fill=1.0,
                             base=0, pattern=[[-1, P]], channel_multiplier=1).then_inc(s_ident, 1)
            gp.memset(neghalf[:, :], -0.5).then_inc(s_const, 1)
            gp.memset(eps[:, :], EPS).then_inc(s_const, 1)
            gp.memset(ceps[:, :], C * EPS).then_inc(s_const, 1)
            gp.memset(mask[:, :], 0.0).then_inc(s_const, 1)
            gp.wait_ge(s_const, 4)
            mv3 = mask[:, :].rearrange("p (j c) -> p j c", c=TOK)
            gp.affine_select(out=mv3, in_=mv3, compare_op=ALU.is_ge, fill=-1e30,
                             base=0, pattern=[[-TOK, BT], [0, TOK]], channel_multiplier=1).then_inc(s_const, 1)
            gp.wait_ge(s_const, 5)
            gp.affine_select(out=mv3, in_=mv3, compare_op=ALU.is_ge, fill=-1e30,
                             base=TOK - 1, pattern=[[TOK, BT], [0, TOK]], channel_multiplier=-1).then_inc(s_const, 1)
            gp.iota(iota[:, :], pattern=[[1, NE]], base=0, channel_multiplier=0,
                    allow_small_or_imprecise_dtypes=True).then_inc(s_const, 1)

            def group(n, idx, g):
                _, _, per, count = g
                gp.wait_ge(ssum_done, n + 1)
                gp.tensor_tensor(varv[0:per, idx, 0:count], ssum[0:per, idx, 0:count], ceps[0:per, 0:count],
                                 ALU.add).then_inc(varv_done, 1)
                gp.wait_ge(varv_done, n + 1)
                gp.tensor_tensor(rstd[0:per, idx, 0:count], varv[0:per, idx, 0:count],
                                 neghalf[0:per, 0:count], ALU.pow).then_inc(rstd_done, 1)

            for k, (_, g) in enumerate(HEAD):
                group(k, k % 4, g)
            with gp.Fori(1, NT) as i:
                for k, (_, g) in enumerate(BODY):
                    group(NHD + (i - 1) * NB + k, (NHD + k) % 4, g)
            for k, (_, g) in enumerate(TAIL):
                group(NHD + (NT - 1) * NB + k, (NHD + k) % 4, g)

            def power(i, tag):
                gp.wait_ge(t["mv" + tag], i + 1)
                gp.tensor_tensor(veps[:, :], mv[:, 1:2], eps[0:M, :], ALU.add).then_inc(t["ve" + tag], 1)
                gp.wait_ge(t["ve" + tag], i + 1)
                gp.tensor_tensor(rs[:, :], veps[:, :], neghalf[0:M, 0:1], ALU.pow).then_inc(t["rs" + tag], 1)

            with gp.Fori(0, NT) as i:
                power(i, "1")
                power(i, "2")
                power(i, "3")

        @block.tensor
        def _(pe):
            pe.wait_ge(s_ident, 2)
            pe.wait_ge(s_w, 16 * 6)
            for q in range(0, NTAP, 4):
                for j in range(4):
                    l, tap = W_TAPS[q + j]
                    k = CONVS[l][0]
                    src = wraw[:, TAP0[l]:TAP0[l] + k, :].rearrange("p t c -> p (t c)")\
                        .rearrange("p (c t) -> p t c", t=k)[:, tap, :]
                    last = nc.tensor.transpose(ps[:, q // 4, j * C:(j + 1) * C], src, ident[:, :])
                last.then_inc(s_wtr, 1)
            pe.wait_ge(s_w0raw, 16)
            nc.tensor.transpose(ps[0:10, 4, 0:C], w0raw[:, :], ident[:, :]).then_inc(s_wtr, 1)
            pe.wait_ge(s_ln, 16 * 16)
            nc.tensor.transpose(ps[:, 5, 0:16], lnraw[:, :], ident[0:16, 0:16]).then_inc(s_wtr, 1)
            pe.wait_ge(s_wt, 5)
            pe.wait_ge(s_pad, 4)
            pe.wait_ge(s_lnc, 1)

            def conv(n, idx, g, seq, k, first, base):
                layer, start, per, count = g
                if not (first and k < YBUF):
                    pe.wait_ge(xh_done, n - YBUF + 1)
                if layer == 0:
                    gi = G0.index(g)
                    pe.wait_ge(s_x[gi % XR], xwait(base, gi))
                    for j in range(count):
                        last = nc.tensor.matmul(y[idx][0:per, j * C:(j + 1) * C],
                                                xr[:, gi % XR, 5 * per * j:5 * per * (j + 1):5], w0t[:, :],
                                                start=True, stop=True)
                    last.then_inc(conv_done, 1)
                    return
                pe.wait_ge(act_done, need(n, g, seq, k))
                taps, st = CONVS[layer]
                for j in range(count):
                    for tap in range(taps):
                        lo = st * (start + per * j) + tap
                        src = h[layer - 1][:, lo:lo + st * (per - 1) + 1:st]
                        last = nc.tensor.matmul(y[idx][0:per, j * C:(j + 1) * C], src, wt[:, TAP0[layer] + tap, :],
                                                start=(tap == 0), stop=(tap == taps - 1))
                last.then_inc(conv_done, 1)

            def xwait(i, gi):
                return (i * (len(G0) // XR) + gi // XR + 1) * 16

            def need(n, g, seq, k):
                d = 0 if g[0] == 1 else 1
                for back in range(1, k + 1):
                    s = seq[k - back]
                    if s[0] == d and feeds(s[1], g):
                        return n - back + 1
                back = min(b for step in (HEAD, BODY) for b, s in enumerate(reversed(step)) if s[0] == 0 and feeds(s[1], g))
                return n - k - back

            def turn(n, idx, g, first, k):
                _, _, per, count = g
                pe.wait_ge(xh_done, n + 1)
                if not (first and k < TRBUF):
                    pe.wait_ge(act_done, n - TRBUF + 1)
                for j in range(count):
                    last = nc.tensor.transpose(tr[idx % TRBUF][:, j * per:(j + 1) * per],
                                               xh[0:per, idx % XHBUF, j * C:(j + 1) * C], ident[0:per, 0:per])
                last.then_inc(tr_done, 1)

            for k, (_, g) in enumerate(HEAD):
                conv(k, k % 4, g, HEAD, k, True, 0)
                if k >= LAG:
                    turn(k - LAG, (k - LAG) % 4, HEAD[k - LAG][1], True, k - LAG)
            with pe.Fori(1, NT) as i:
                for k, (_, g) in enumerate(BODY):
                    n = NHD + (i - 1) * NB + k
                    conv(n, (NHD + k) % 4, g, BODY, k, False, i)
                    before = BODY[k - LAG][1] if k >= LAG else None
                    if k < LAG:
                        before = BODY[k - LAG][1]
                    turn(n - LAG, (NHD + k - LAG) % 4, before, False, k)
            assert [s[1] for s in HEAD[-LAG:]] == [s[1] for s in BODY[-LAG:]]
            assert all(s[0] == 0 for s in BODY[-LAG:])
            base = NHD + (NT - 1) * NB
            for now, before in zip(ENDING[LAG:], ENDING):
                if now:
                    conv(base + now[0], (NHD + now[0]) % 4, now[1], TAIL, now[0], False, NT)
                if before:
                    turn(base + before[0], (NHD + before[0]) % 4, before[1], False, 0)

            pe.wait_ge(s_tw, 16 * 10)
            pe.wait_ge(s_pad, 8)
            with pe.Fori(0, NT) as i:
                pe.wait_ge(t["h6c"], i + 1)
                nc.tensor.transpose(pa[0:M, 0:C], act[:, 0, :], ident[:, :]).then_inc(t["h6r"], 1)
                pe.wait_ge(t["xh1"], i + 1)
                nc.tensor.transpose(pb[:, 0:M], xn[:, 0:C], ident[0:M, 0:M]).then_inc(t["xhT"], 1)
                pe.wait_ge(t["a1"], i + 1)
                nc.tensor.matmul(pa[0:M, 0:D], act[:, 0, :], projw[:, :], start=True, stop=False)
                nc.tensor.matmul(pa[0:M, 0:D], ones[0:1, 0:M], projb[0:1, :], start=False, stop=True).then_inc(t["pj"], 1)

                def turn2(src, ready, done):
                    pe.wait_ge(ready, i + 1)
                    nc.tensor.transpose(pb[:, 0:M], src[:, 0:P], ident[0:M, 0:M])
                    nc.tensor.transpose(pb[0:D1, M:2 * M], src[:, P:D], ident[0:M, 0:M]).then_inc(done, 1)

                turn2(xn, t["xn2"], t["xn2T"])
                pe.wait_ge(t["a2"], i + 1)
                for j in range(4):
                    lo = (j // 2) * D + (j % 2) * P
                    w = D1 if j % 2 else P
                    nc.tensor.matmul(pa[0:w, j * M:(j + 1) * M], wqkv[:, 0, lo:lo + w], act[:, 0, :], start=True, stop=False)
                    nc.tensor.matmul(pa[0:w, j * M:(j + 1) * M], wqkv[0:D1, 1, lo:lo + w], act[0:D1, 1, :], start=False, stop=True)
                nc.tensor.matmul(pb[0:M, 0:D], act[:, 0, :], wqkv[:, 0, 2 * D:3 * D], start=True, stop=False)
                nc.tensor.matmul(pb[0:M, 0:D], act[0:D1, 1, :], wqkv[0:D1, 1, 2 * D:3 * D], start=False, stop=True).then_inc(t["qkv"], 1)
                pe.wait_ge(t["qk"], i + 1)
                for hd in range(NH):
                    rows = P if hd < 4 else D1
                    last = nc.tensor.matmul((pa, pb)[hd // 3][0:M, (hd % 3) * M:(hd % 3 + 1) * M], qm[0:rows, hd, :],
                                            kT[0:rows, hd // 4, :], start=True, stop=True)
                last.then_inc(t["sc"], 1)
                pe.wait_ge(t["ex"], i + 1)
                for hd in range(NH):
                    last = nc.tensor.transpose((pa, pb)[hd // 3][0:M, (hd % 3) * M:(hd % 3 + 1) * M], t1[:, hd, :], ident[0:M, 0:M])
                last.then_inc(t["pT"], 1)
                pe.wait_ge(t["pTc"], i + 1)
                for hd in range(NH):
                    last = nc.tensor.matmul(pa[0:M, hd * HD:(hd + 1) * HD], pT[:, hd, :], vv[:, hd * HD:(hd + 1) * HD],
                                            start=True, stop=True)
                last.then_inc(t["pv"], 1)
                turn2(oo, t["oo"], t["ooT"])
                pe.wait_ge(t["a3"], i + 1)
                nc.tensor.matmul(pa[0:M, 0:D], act[:, 0, :], wprj[:, 0, :], start=True, stop=False)
                nc.tensor.matmul(pa[0:M, 0:D], act[0:D1, 1, :], wprj[0:D1, 1, :], start=False, stop=True).then_inc(t["at"], 1)
                turn2(xn, t["xn3"], t["xn3T"])
                pe.wait_ge(t["a4"], i + 1)
                nc.tensor.matmul(pb[0:M, 0:NE], act[:, 0, :], wsr[:, 0, :], start=True, stop=False)
                nc.tensor.matmul(pb[0:M, 0:NE], act[0:D1 + 1, 1, :], wsr[0:D1 + 1, 1, :], start=False, stop=True).then_inc(t["lo"], 1)
                pe.wait_ge(t["lg"], i + 1)

            def up(n, e2, tt, first):
                for half in range(2):
                    o = ps[0:M, 2 * (tt % 2) + half, 0:DFF // 2]
                    nc.tensor.matmul(o, xt[:, tt * M:(tt + 1) * M], W1s[:, e2, half * 384:(half + 1) * 384], start=True, stop=False)
                    last = nc.tensor.matmul(o, xtb[:, tt * M:(tt + 1) * M], W1b[:, e2, half * 384:(half + 1) * 384], start=False, stop=True)
                last.then_inc(f_h, 1)

            def down(n, b2, e2, tt, first):
                pe.wait_ge(f_g, n + 1)
                if not first:
                    pe.wait_ge(f_c, n)
                for f in range(NF):
                    last = nc.tensor.transpose(ps[:, 4 + f // 3, (f % 3) * M:(f % 3 + 1) * M], hs[:, tt % 2, f * P:(f + 1) * P], ident[0:M, 0:M])
                last.then_inc(f_t, 1)

            def fin(n, b2, e2, tt, first):
                pe.wait_ge(f_c, n + 1)
                if not first:
                    pe.wait_ge(f_acc, n - 1)
                o = ps[0:M, 6 + tt % 2, 0:D]
                for f in range(NF):
                    nc.tensor.matmul(o, hT[:, tt % 2, f // 3, (f % 3) * M:(f % 3 + 1) * M], W2s[:, e2, f, :], start=(f == 0), stop=False)
                nc.tensor.matmul(o, ones[0:1, 0:M], b2, start=False, stop=True).then_inc(f_o, 1)

            pe.wait_ge(t["coef"], NT)
            for e in range(NE):
                pe.wait_ge(f_w[e % 2], 16 * 4 * (e // 2 + 1))
                b2 = b2s[0:1, e * D:(e + 1) * D]
                for tt in range(NT):
                    n = e * NT + tt
                    if n >= 2:
                        pe.wait_ge(f_g, n - 1)
                    up(n, e % 2, tt, False)
                    if tt:
                        down(n - 1, b2, e % 2, tt - 1, n - 1 == 0)
                        fin(n - 1, b2, e % 2, tt - 1, n - 1 < 2)
                down(n, b2, e % 2, NT - 1, False)
                fin(n, b2, e % 2, NT - 1, False)

        @block.vector
        def _(ve):
            for l in range(4):
                nc.vector.memset(h[l][:, FLAT[l]:FLAT[l] + 1], 0.0).then_inc(s_pad, 1)
            nc.vector.memset(ones[:, :], 1.0).then_inc(s_pad, 1)
            nc.vector.memset(xtb[D1:D1 + 1, :], 1.0).then_inc(s_pad, 1)
            nc.vector.memset(act[D1:D1 + 1, 1, :], 1.0).then_inc(s_pad, 1)
            nc.vector.memset(qm[:, :, :], 0.0).then_inc(s_pad, 1)
            for q in range(5):
                ve.wait_ge(s_wtr, q + 1)
                rows, cnt = (P, 4) if q < 4 else (10, 1)
                src = ps[0:rows, q, 0:cnt * C].rearrange("p (t c) -> p t c", c=C)
                dst = wt[:, 4 * q:4 * q + 4, :] if q < 4 else w0t[:, :].rearrange("p (t c) -> p t c", t=1)
                if q:
                    ve.wait_ge(s_wt, q)
                nc.vector.reduce_sum(wmean[0:rows, 0:cnt], src, axis=X).then_inc(s_wmean, 1)
                ve.wait_ge(s_wmean, q + 1)
                nc.vector.tensor_scalar(wscaled[0:rows, 0:cnt], wmean[0:rows, 0:cnt], 1.0 / C, None,
                                        ALU.mult).then_inc(s_wscaled, 1)
                ve.wait_ge(s_wscaled, q + 1)
                for j in range(cnt):
                    last = nc.vector.tensor_scalar(dst[:, j, :], src[:, j, :], wscaled[0:rows, j:j + 1], None, ALU.subtract)
                last.then_inc(s_wt, 1)
            ve.wait_ge(s_wtr, 6)
            nc.vector.tensor_copy(lncol[:, 7:16], ps[:, 5, 7:16])
            nc.vector.tensor_scalar(lncol[:, 0:7], ps[:, 5, 0:7], float(C) ** 0.5, None, ALU.mult).then_inc(s_lnc, 1)

            def group(n, idx, g, early):
                _, _, per, count = g
                w = count * C
                ve.wait_ge(sq_done, n + 1)
                nc.vector.reduce_sum(ssum[0:per, idx, 0:count],
                                     sq[0:per, idx % SQBUF, 0:w].rearrange("p (j c) -> p j c", c=C), axis=X).then_inc(ssum_done, 1)

            def norm(n, idx, g, early):
                _, _, per, count = g
                w = count * C
                ve.wait_ge(rstd_done, n + 1)
                if not early:
                    ve.wait_ge(tr_done, n - XHBUF + 1)
                nc.vector.tensor_tensor(xh[0:per, idx % XHBUF, 0:w].rearrange("p (j c) -> p j c", c=C),
                                        y[idx][0:per, 0:w].rearrange("p (j c) -> p j c", c=C),
                                        rstd[0:per, idx, 0:count].unsqueeze(2).to_broadcast([per, count, C]),
                                        ALU.mult).then_inc(xh_done, 1)

            for k, (_, g) in enumerate(HEAD):
                group(k, k % 4, g, k < XHBUF)
                if k >= 1:
                    norm(k - 1, (k - 1) % 4, HEAD[k - 1][1], k - 1 < XHBUF)
            with ve.Fori(1, NT) as i:
                for k, (_, g) in enumerate(BODY):
                    n = NHD + (i - 1) * NB + k
                    group(n, (NHD + k) % 4, g, False)
                    norm(n - 1, (NHD + k - 1) % 4, BODY[k - 1][1], False)
            base = NHD + (NT - 1) * NB
            for now, before in zip(ENDING[LAG:], ENDING[LAG - 1:]):
                if now:
                    group(base + now[0], (NHD + now[0]) % 4, now[1], False)
                if before:
                    norm(base + before[0], (NHD + before[0]) % 4, before[1], False)

            with ve.Fori(0, NT) as i:
                def stat(src, tag, wait):
                    if wait is not None:
                        ve.wait_ge(wait, i + 1)
                    nc.vector.bn_stats(stats[:, :], src).then_inc(t["st" + tag], 1)
                    ve.wait_ge(s_pad, 8)
                    ve.wait_ge(t["st" + tag], i + 1)
                    nc.vector.bn_aggr(mv[:, :], stats[:, :]).then_inc(t["mv" + tag], 1)

                def normed(dst, src, tag, done):
                    ve.wait_ge(t["rs" + tag], i + 1)
                    nc.vector.tensor_scalar(dst, src, mv[:, 0:1], rs[:, 0:1], ALU.subtract, ALU.mult).then_inc(done, 1)

                stat(pa[0:M, 0:C], "1", t["h6r"])
                normed(xn[:, 0:C], pa[0:M, 0:C], "1", t["xh1"])
                ve.wait_ge(t["pj"], i + 1)
                nc.vector.tensor_copy(x1[:, :], pa[0:M, 0:D]).then_inc(t["x1"], 1)
                stat(x1[:, :], "2", t["x1"])
                normed(xn[:, :], x1[:, :], "2", t["xn2"])
                ve.wait_ge(t["qkv"], i + 1)
                for hd in range(NH):
                    r = (hd % 4) * HD
                    nc.vector.tensor_copy(qm[r:r + HD, hd, :], pa[r:r + HD, (hd // 4) * M:(hd // 4 + 1) * M])
                nc.vector.tensor_copy(kT[:, 0, :], pa[:, 2 * M:3 * M])
                nc.vector.tensor_copy(kT[0:D1, 1, :], pa[0:D1, 3 * M:4 * M])
                nc.vector.tensor_copy(vv[:, :], pb[0:M, 0:D]).then_inc(t["qk"], 1)
                ve.wait_ge(t["sc"], i + 1)
                for half in range(2):
                    last = nc.vector.tensor_tensor(t1[:, 3 * half:3 * half + 3, :],
                                                   (pa, pb)[half][0:M, 0:3 * M].rearrange("p (h k) -> p h k", h=3),
                                                   mask[:, :].unsqueeze(1).to_broadcast([M, 3, M]), ALU.add)
                last.then_inc(t["msk"], 1)
                ve.wait_ge(t["msk"], i + 1)
                nc.vector.reduce_max(mx[:, :], t1[:, :, :], axis=X).then_inc(t["mx"], 1)
                ve.wait_ge(t["mx"], i + 1)
                nc.vector.tensor_tensor(t1[:, :, :], t1[:, :, :], mx[:, :].unsqueeze(2).to_broadcast([M, NH, M]),
                                        ALU.subtract).then_inc(t["sub"], 1)
                ve.wait_ge(t["ex"], i + 1)
                nc.vector.reduce_sum(den[:, :], t1[:, :, :], axis=X).then_inc(t["den"], 1)
                ve.wait_ge(t["den"], i + 1)
                nc.vector.reciprocal(rden[:, :], den[:, :]).then_inc(t["rden"], 1)
                ve.wait_ge(t["rden"], i + 1)
                ve.wait_ge(t["pT"], i + 1)
                for half in range(2):
                    last = nc.vector.tensor_copy(pT[:, 3 * half:3 * half + 3, :],
                                                 (pa, pb)[half][0:M, 0:3 * M].rearrange("p (h k) -> p h k", h=3))
                last.then_inc(t["pTc"], 1)
                ve.wait_ge(t["pv"], i + 1)
                nc.vector.tensor_tensor(oo[:, :].rearrange("p (h d) -> p h d", h=NH),
                                        pa[0:M, 0:D].rearrange("p (h d) -> p h d", h=NH),
                                        rden[:, :].unsqueeze(2).to_broadcast([M, NH, HD]), ALU.mult).then_inc(t["oo"], 1)
                ve.wait_ge(t["at"], i + 1)
                nc.vector.tensor_tensor(x1[:, :], pa[0:M, 0:D], x1[:, :], ALU.add).then_inc(t["x2"], 1)
                ve.wait_ge(t["x2"], i + 1)
                nc.vector.tensor_copy(acc[:, bass.ds(i, 1), :], x1[:, :].unsqueeze(1))
                stat(x1[:, :], "3", None)
                normed(xn[:, :], x1[:, :], "3", t["xn3"])
                ve.wait_ge(t["lo"], i + 1)
                nc.vector.tensor_copy(lg[:, :], pb[0:M, 0:NE]).then_inc(t["lg"], 1)
                ve.wait_ge(t["lg"], i + 1)
                nc.vector.reduce_max(s1[:, 0:1], lg[:, :], axis=X).then_inc(t["mxl"], 1)
                ve.wait_ge(t["mxl"], i + 1)
                nc.vector.tensor_scalar(lgt[:, :], lg[:, :], s1[:, 0:1], None, ALU.subtract).then_inc(t["subl"], 1)
                nc.vector.tensor_scalar(lg[:, :], lg[:, :], s1[:, 0:1], 100.0, ALU.is_lt, ALU.mult).then_inc(t["pmax"], 1)
                ve.wait_ge(t["pmax"], i + 1)
                nc.vector.tensor_tensor(lg[:, :], lg[:, :], iota[:, :], ALU.add).then_inc(t["cand"], 1)
                ve.wait_ge(t["cand"], i + 1)
                nc.vector.tensor_reduce(s1[:, 1:2], lg[:, :], axis=X, op=ALU.min).then_inc(t["first"], 1)
                ve.wait_ge(t["exl"], i + 1)
                nc.vector.reduce_sum(s1[:, 2:3], lgt[:, :], axis=X).then_inc(t["suml"], 1)
                ve.wait_ge(t["suml"], i + 1)
                ve.wait_ge(t["first"], i + 1)
                nc.vector.reciprocal(s1[:, 3:4], s1[:, 2:3]).then_inc(t["hot"], 1)
                ve.wait_ge(t["hot"], i + 1)
                nc.vector.tensor_scalar(lg[:, :], iota[:, :], s1[:, 1:2], s1[:, 3:4], ALU.is_equal, ALU.mult)
                nc.vector.tensor_scalar(s1[:, 4:5], s1[:, 3:4], -1.0, 1.0, ALU.mult, ALU.add).then_inc(s_shares, 1)
                ve.wait_ge(s_shares, i + 1)
                nc.vector.tensor_copy(coef[:, 1:NE, bass.ds(i, 1)], lg[:, 1:NE].unsqueeze(2))
                nc.vector.tensor_scalar(coef[:, 0:1, bass.ds(i, 1)], lg[:, 0:1].unsqueeze(2), s1[:, 4:5], None, ALU.add).then_inc(t["coef"], 1)
            ve.wait_ge(t["coef"], NT)

            def combine(n):
                e, tt = n // NT, n % NT
                ve.wait_ge(f_o, n + 1)
                if n >= NT:
                    ve.wait_ge(f_acc, n - NT + 1)
                nc.vector.scalar_tensor_tensor(out=acc[:, tt, :], in0=ps[0:M, 6 + tt % 2, 0:D], scalar=coef[:, e, tt:tt + 1],
                                               in1=acc[:, tt, :], op0=ALU.mult, op1=ALU.add).then_inc(f_acc, 1)

            for e in range(NE):
                for tt in range(NT):
                    n = e * NT + tt
                    ve.wait_ge(f_t, n + 1)
                    if n >= 2:
                        ve.wait_ge(f_o, n - 1)
                    nc.vector.tensor_copy(hT[:, tt % 2, :, :], ps[:, 4:6, 0:3 * M]).then_inc(f_c, 1)
                    if n >= 1:
                        combine(n - 1)
            combine(NE * NT - 1)

        @block.scalar
        def _(ac):
            def tload(dst, src):
                ac.dma_start(dst, src).then_inc(s_tw, 16)
            tload(projw[:, :], a["L0_tok_proj_w"])
            tload(projb[:, :], a["L0_tok_proj_b"].rearrange("(a c) -> a c", a=1))
            for src, dst, n in ((a["L0_attn_w_qkv"], wqkv, 3 * D), (a["L0_attn_w_proj"], wprj, D), (a["L0_ffn_Ws"], wsr, NE)):
                tload(dst[:, 0, :], src[0:P, :])
                tload(dst[0:D1, 1, :], src[P:D, :])
            tload(wsr[D1:D1 + 1, 1, :], a["L0_ffn_bs"].rearrange("(a c) -> a c", a=1))
            tload(b2s[:, :], a["L0_ffn_b2"].rearrange("e d -> (e d)").rearrange("(a c) -> a c", a=1))

            ac.wait_ge(s_lnc, 1)

            def square(n, idx, g, early):
                _, _, per, count = g
                w = count * C
                ac.wait_ge(conv_done, n + 1)
                if not early:
                    ac.wait_ge(ssum_done, n - SQBUF + 1)
                nc.scalar.activation(sq[0:per, idx % SQBUF, 0:w], y[idx][0:per, 0:w], ACT.Square).then_inc(sq_done, 1)

            def gelu(n, idx, g, i):
                layer, start, per, count = g
                w = count * per
                ac.wait_ge(tr_done, n + 1)
                src = tr[idx % TRBUF][:, 0:w]
                if layer == 6:
                    dst = h6[:, bass.ds(i * M, M)]
                elif layer == 5:
                    src = src.rearrange("p (b q) -> p b q", b=BT)[:, :, 0:LAST5]
                    dst = h[5][:, :].rearrange("p (b q) -> p b q", b=BT)
                else:
                    dst = h[layer][:, start:start + w]
                nc.scalar.activation(dst, src, ACT.Gelu, bias=lncol[:, 8 + layer:9 + layer],
                                     scale=lncol[:, layer:layer + 1]).then_inc(act_done, 1)

            for k, (_, g) in enumerate(HEAD):
                square(k, k % 4, g, k < SQBUF)
                if k >= LAG:
                    gelu(k - LAG, (k - LAG) % 4, HEAD[k - LAG][1], None)
            with ac.Fori(1, NT) as i:
                for k, (_, g) in enumerate(BODY):
                    n = NHD + (i - 1) * NB + k
                    square(n, (NHD + k) % 4, g, False)
                    gelu(n - LAG, (NHD + k - LAG) % 4, BODY[k - LAG][1], i - 1)
            base = NHD + (NT - 1) * NB
            for now, before in zip(ENDING[LAG:], ENDING):
                if now:
                    square(base + now[0], (NHD + now[0]) % 4, now[1], False)
                if before:
                    gelu(base + before[0], (NHD + before[0]) % 4, before[1], NT - 1)

            with ac.Fori(0, NT) as i:
                ac.wait_ge(act_done, NG)
                nc.scalar.copy(act[:, 0, :], h6[:, bass.ds(i * M, M)]).then_inc(t["h6c"], 1)
                ac.wait_ge(t["xhT"], i + 1)
                nc.scalar.activation(act[:, 0, :], pb[:, 0:M], ACT.Identity, bias=lncol[:, 15:16], scale=lncol[:, 7:8]).then_inc(t["a1"], 1)

                def copy2(wait, done):
                    ac.wait_ge(wait, i + 1)
                    nc.scalar.copy(act[:, 0, :], pb[:, 0:M])
                    nc.scalar.copy(act[0:D1, 1, :], pb[0:D1, M:2 * M]).then_inc(done, 1)

                copy2(t["xn2T"], t["a2"])
                ac.wait_ge(t["sub"], i + 1)
                nc.scalar.activation(t1[:, :, :], t1[:, :, :], ACT.Exp, scale=SCALE).then_inc(t["ex"], 1)
                copy2(t["ooT"], t["a3"])
                ac.wait_ge(t["xn3T"], i + 1)
                nc.scalar.copy(xt[:, bass.ds(i * M, M)], pb[:, 0:M])
                nc.scalar.copy(act[:, 0, :], pb[:, 0:M])
                nc.scalar.copy(act[0:D1, 1, :], pb[0:D1, M:2 * M])
                nc.scalar.copy(xtb[0:D1, bass.ds(i * M, M)], pb[0:D1, M:2 * M]).then_inc(t["a4"], 1)
                ac.wait_ge(t["subl"], i + 1)
                nc.scalar.activation(lgt[:, :], lgt[:, :], ACT.Exp).then_inc(t["exl"], 1)
            for e in range(NE):
                for tt in range(NT):
                    n = e * NT + tt
                    ac.wait_ge(f_h, n + 1)
                    if n >= 2:
                        ac.wait_ge(f_t, n - 1)
                    nc.scalar.activation(hs[:, tt % 2, :].rearrange("p (a b) -> p a b", a=2),
                                         ps[0:M, 2 * (tt % 2):2 * (tt % 2) + 2, 0:DFF // 2], ACT.Gelu).then_inc(f_g, 1)


_OUTS = [((64, 12, 192), "float32")]


def kernel(**inputs):
    import numpy as _np
    import concourse.bacc as _bacc
    from concourse import mybir as _mybir
    from concourse.bass_utils import run_bass_kernel_spmd as _run

    nc = _bacc.Bacc("TRN2", target_bir_lowering=False, num_devices=1)
    arrays, args = {}, {}
    for name in inputs:
        a = _np.ascontiguousarray(inputs[name])
        arrays[f"in_{name}_dram"] = a
        args[name] = nc.dram_tensor(f"in_{name}_dram", a.shape, _mybir.dt.from_np(a.dtype), kind="ExternalInput").ap()
    outs = []
    for i, (shape, dtype) in enumerate(_OUTS):
        outs.append(nc.dram_tensor(f"out_{i}_dram", shape, _mybir.dt.from_np(_np.dtype(dtype)), kind="ExternalOutput").ap())
    audio_tower(nc, args, outs[0])
    r = _run(nc, [arrays], core_ids=[0])
    return r.results[0]["out_0_dram"]
```

```python
import numpy as np
import concourse.bass as bass
from concourse import mybir
from contextlib import ExitStack

F32 = mybir.dt.float32
F32R = mybir.dt.float32r
ALU = mybir.AluOpType
ACT = mybir.ActivationFunctionType
X = mybir.AxisListType.X

P = 128
BATCH, SAMPLES = 64, 4000
C = 128
CONVS = [(10, 5), (3, 2), (3, 2), (3, 2), (3, 2), (2, 2), (2, 2)]
NT = 8
BT = BATCH // NT
D = 192
D1 = D - P
TOK = 12
M = BT * TOK
NH, HD = 6, 32
DFF, NE = 768, 9
NF = DFF // P
EPS = 1e-5
SCALE = float(HD) ** -0.5
TOKENS = BATCH * TOK
NTILE = (NE - 1) + (TOKENS - (NE - 1)) // P
ROWS = NTILE * P + TOKENS
WR = 2

PITCH = [800, 400, 200, 100, 50, 25, 12]
FLAT = [BT * p for p in PITCH]
LAST5 = 24

def cut(layer, per, counts, start=0):
    out = []
    for c in counts:
        out.append((layer, start, per, c))
        start += per * c
    return out

G0 = cut(0, 128, [3] * 14 + [4] * 2)
G1 = cut(1, 128, [4] * 4 + [3] * 3)
G2 = cut(2, 128, [4] * 2) + cut(2, 96, [3] * 2, 1024)
G3 = cut(3, 128, [4]) + cut(3, 96, [3], 512)
G4 = cut(4, 100, [4])
G5 = cut(5, 100, [2])
G6 = cut(6, M, [1])
GROUPS = [G0, G1, G2, G3, G4, G5, G6]
DELAY = [0, 1, 1, 2, 2, 2, 2]
ORDER = [1, 0, 1, 0, 3, 0, 3, 0, 0, 1, 0, 1, 0, 0, 1, 0, 1, 0, 2, 4, 0, 2, 1, 0, 5, 0, 0, 2, 6, 0, 2, 0]
LAG = 3
YBUF, SQBUF, XHBUF, TRBUF, XR = 4, 2, 2, 2, 4


def reads(group):
    layer, start, per, count = group
    if layer == 0:
        return 0, 0
    k, s = CONVS[layer]
    if layer == 6:
        return 0, FLAT[5]
    return s * start, min(s * (start + per * count - 1) + k, FLAT[layer - 1])


def feeds(a, b):
    lo, hi = reads(b)
    return a[0] == b[0] - 1 and a[1] < hi and a[1] + a[2] * a[3] > lo


BODY = [(DELAY[l], GROUPS[l][ORDER[:k].count(l)]) for k, l in enumerate(ORDER)]
assert all(ORDER.count(l) == len(GROUPS[l]) for l in range(7))
NB = len(BODY)
assert NB % 4 == 0, NB
HEAD = [(0, g) for g in G0] + [(1 - d, g) for d, g in BODY if d <= 1]
NHD = len(HEAD)
LOOP = [(i - d, g) for i in range(2, NT) for d, g in BODY]
TAIL = [(NT - d, g) for d, g in BODY if d >= 1] + [(NT + 1 - d, g) for d, g in BODY if d == 2]
ALL = HEAD + LOOP + TAIL
NG = len(ALL)
assert [s[1] for s in HEAD[-LAG:]] == [s[1] for s in BODY[-LAG:]]


def last_feed(n):
    return max((m for m in range(n) if ALL[m][0] == ALL[n][0] and feeds(ALL[m][1], ALL[n][1])), default=None)


BACK = [None if g[0] == 0 else min(n - last_feed(n) for n in range(NHD + k, NG - len(TAIL), NB))
        for k, (_, g) in enumerate(BODY)]
assert all(b is None or b > LAG for b in BACK)
for w, (tile, g) in enumerate(ALL):
    assert all(r <= w + LAG for r, s in enumerate(ALL) if s[0] == tile - 1 and feeds(g, s[1])), (w, g)
H6_BACK = NB - ORDER.index(6)


SLOT = {"turn_h": 0, "stat_h": 1, "power_h": 1, "norm_h": 2, "turn_norm_h": 4, "affine_h": 4, "project": 6,
        "stat_1": 7, "power_1": 7, "norm_1": 8, "turn_1": 9, "copy_1": 9, "qkv": 11, "split_heads": 12,
        "scores": 14, "mask": 15, "less_max": 16, "exp": 17, "turn_probs": 18, "copy_probs": 18, "values": 19,
        "divide": 20, "turn_heads": 21, "copy_heads": 21, "out_project": 22, "residual": 23, "power_2": 23,
        "norm_2": 24, "turn_2": 27, "copy_2": 27, "logits": 30, "keep_logits": 31}
STEPS = list(SLOT)
AT = [[step for step in STEPS if SLOT[step] == k] for k in range(NB)]
RUNS = NT + 1
PER_SLOT = 2


def spread():
    slots = list(range(NG - len(TAIL) - LAG, NG - len(TAIL)))
    for n in range(NG - len(TAIL), NG):
        while slots[-LAG:].count(last_feed(n)):
            slots.append(None)
        slots.append(n)
    return slots + [None] * LAG


ENDING = spread()
NE_SLOTS = len(ENDING) - LAG
LAST_STEPS = [[] for _ in range(NE_SLOTS)]
free = 0
for run, n6 in ((NT - 2, None), (NT - 1, max(n for n, s in enumerate(ALL) if s == (NT - 2, G6[0]))), (NT, NG - 1)):
    if n6 is not None:
        free = max(free, ENDING.index(n6) + 1)
    last_run = free
    for k, step in enumerate(STEPS):
        while len(LAST_STEPS) <= free:
            LAST_STEPS.append([])
        LAST_STEPS[free].append((step, run))
        if k % PER_SLOT == PER_SLOT - 1:
            free += 1
HALF = NT // 2
COMMON_AT = [last_run + 1 + k for k in range(NF)] + [last_run + 2 + NF + k for k in range(HALF)]
COMMON_BANK = [(4, 5, 0, 1)[i % 4] for i in range(NT)]
while len(LAST_STEPS) < COMMON_AT[-1] + 2:
    LAST_STEPS.append([])
XPP = BT * SAMPLES // P
XBLOCKS = ((0, 1), (1, 2), (2, NT))
K0 = CONVS[0][0]
XCOLS = [max(5 * g[2] * g[3] for g in G0[r::XR]) for r in range(XR)]
W_TAPS = [(l, t) for l in range(1, 7) for t in range(CONVS[l][0])]
TAP0 = {l: W_TAPS.index((l, 0)) for l in range(1, 7)}
NTAP = len(W_TAPS)
TAPS_AT = (5, 7, 9, 11)
assert NTAP == 4 * len(TAPS_AT)


def audio_tower(nc, a, out):
    ctx = ExitStack()
    with ctx:
        def sb(name, shape, dt=F32):
            return ctx.enter_context(nc.sbuf_tensor(name, shape, dt))

        def sem(name):
            return ctx.enter_context(nc.semaphore(name))

        h = [sb(f"h{l}", [P, FLAT[l] + (l < 4) if l < 5 else BT * LAST5]) for l in range(6)]
        h6 = sb("h6", [P, M])
        xring = sb("xring", [4 * K0, sum(XCOLS)], F32R)
        xr = [xring[:, sum(XCOLS[:r]):sum(XCOLS[:r + 1])] for r in range(XR)]
        w0t = sb("w0t", [4 * K0, C], F32R)
        w0c = sb("w0c", [4 * K0, C])
        w0h = sb("w0h", [4 * K0, C], F32R)
        w0m = sb("w0m", [4 * K0, 2])
        wt = sb("wt", [P, NTAP, C])
        wraw = h[1][:, 0:NTAP * C].rearrange("p (t c) -> p t c", c=C)
        w0raw = sb("w0raw", [P, 4, K0])
        lnraw = sb("lnraw", [16, C])
        lncol = sb("lncol", [P, 16])
        wmean = sb("wmean", [P, 4])
        wscaled = sb("wscaled", [P, 4])
        ident = sb("ident", [P, P])
        mask = sb("mask", [M, M])
        r0 = sb("r0", [1, 1])
        neghalf = sb("neghalf", [P, 4])
        eps = sb("eps", [P, 1])
        ceps = sb("ceps", [P, 4])
        sq = sb("sq", [P, SQBUF, 512])
        xh = sb("xh", [P, XHBUF, 512])
        ssum = sb("ssum", [P, YBUF, 4])
        varv = sb("varv", [P, YBUF, 4])
        rstd = sb("rstd", [P, YBUF, 4])

        projw = sb("projw", [P, D])
        projb = sb("projb", [1, D])
        wqkv = sb("wqkv", [P, 2, 3 * D])
        wprj = sb("wprj", [P, 2, D])
        wsr = sb("wsr", [P, 2, NE])
        ones = sb("ones", [1, P])
        iota = sb("iota", [M, NE])
        W1c = sb("W1c", [P, DFF])
        W1cb = sb("W1cb", [D1 + 1, DFF])
        W1r = h[1][:, 0:WR * DFF].rearrange("p (r c) -> p r c", r=WR)
        W1rb = h[1][0:D1 + 1, WR * DFF:2 * WR * DFF].rearrange("p (r c) -> p r c", r=WR)
        W2s = sb("W2s", [P, NE, NF, D])
        b2c = sb("b2c", [1, D])
        b2s = wt[0:1, :, :].rearrange("p t c -> p (t c)")[:, 0:NE * D]
        flat2 = W2s[:, :, :, :].rearrange("p e f d -> p (e f d)")
        xraw, xhi, xlo = (flat2[:, j * NT * XPP:(j + 1) * NT * XPP] for j in range(3))
        xt_ = sb("xt", [P, RUNS * M])
        xtb_ = sb("xtb", [D1 + 1, RUNS * M])
        acc_ = sb("acc", [M, RUNS, D])
        xt, xtb, acc = xt_[:, M:RUNS * M], xtb_[:, M:RUNS * M], acc_[:, 1:RUNS, :]

        stats = sb("stats", [M, 6])
        mv = sb("mv", [M, 2])
        veps = sb("veps", [M, 1])
        rs = sb("rs", [M, 1])
        xn = sb("xn", [M, D])
        act = sb("act", [P, 2, M])
        x1 = sb("x1", [M, D])
        qm = sb("qm", [P, NH, M])
        kT = sb("kT", [P, 2, M])
        vv = sb("vv", [M, D])
        t1 = sb("t1", [M, NH, M])
        mx = sb("mx", [M, NH])
        den = sb("den", [M, NH])
        rden = sb("rden", [M, NH])
        pT = sb("pT", [M, NH, M])
        oo = sb("oo", [M, D])
        hc = h[0][:, 0:NF * TOKENS].rearrange("p (f t) -> p f t", f=NF)
        kept = sq[:, :, :].rearrange("p b c -> p (b c)")[0:M, 0:HALF * D].rearrange("p (i d) -> p i d", i=HALF)
        ht = h[2][:, 0:2 * DFF].rearrange("p (b f) -> p b f", b=2)
        xs = h[3][:, 0:2 * D].rearrange("p (b d) -> p b d", b=2)
        xst = h[3][:, 2 * D:2 * D + 2 * P].rearrange("p (b t) -> p b t", b=2)
        xstb = sb("xstb", [D1 + 1, 2, P])
        ysb = h[4][:, 0:2 * D].rearrange("p (b d) -> p b d", b=2)
        sel = h[0][0:M, NF * TOKENS:NF * TOKENS + NT * D].rearrange("p (i d) -> p i d", i=NT)
        xn3_ = sb("xn3", [M, RUNS, D])
        xn3 = xn3_[:, 1:RUNS, :]
        zero = sb("zero", [P, D])
        lga_ = sb("lga", [M, RUNS, NE])
        lga = lga_[:, 1:RUNS, :]
        lgb = sb("lgb", [M, NT, NE])
        hot = sb("hot", [M, NT, NE])
        r8 = sb("r8", [M, 8, NT])
        c0 = sb("c0", [M, NT])
        upper = sb("upper", [M, M])
        onesm = sb("onesm", [M, M])
        full = sb("full", [M, NE, TOKENS // P])
        below = sb("below", [M, NE, NE])
        dump = sb("dump", [M, NE])
        jota = sb("jota", [1, NTILE, NE])
        tiles3 = sb("tiles3", [M, NE, TOKENS // P])
        tiles = sb("tiles", [M, NE])
        base3 = sb("base3", [M, NE, NE])
        basev = sb("basev", [M, NE])
        base2 = sb("base2", [M, NE])
        upto = sb("upto", [1, NE])
        own3 = sb("own3", [1, NTILE, NE])
        ownf = sb("ownf", [1, NTILE])
        owni = sb("owni", [1, NTILE], mybir.dt.int32)
        slotf = sb("slotf", [M, NT])
        sloti = sb("sloti", [M, NT], mybir.dt.uint32)
        xparts = nc.dram_tensor("sample_parts", [4, BATCH * SAMPLES], F32, kind="Internal").ap()
        xs_dram = nc.dram_tensor("sorted_tokens", [ROWS, D], F32, kind="Internal").ap()
        ys_dram = nc.dram_tensor("sorted_results", [ROWS, D], F32, kind="Internal").ap()

        ps = ctx.enter_context(nc.psum_tensor("ps", [P, 8, 512], F32))
        y = [ps[:, i, :] for i in range(4)]
        tr = [ps[:, 4 + i, :] for i in range(2)]
        pa, pb = ps[:, 6, :], ps[:, 7, :]

        s_w = sem("s_w")
        s_ln = sem("s_ln")
        s_ident = sem("s_ident")
        s_const = sem("s_const")
        s_w0raw = sem("s_w0raw")
        s_xraw = [sem(f"samples_here{b}") for b in range(len(XBLOCKS))]
        s_stored = [sem(f"parts_stored{b}") for b in range(len(XBLOCKS))]
        s_high = sem("high_parts")
        s_parts = sem("both_parts")
        s_w0m = sem("w0_masks")
        s_w0s = sem("w0_steps")
        s_w0t = sem("w0_ready")
        s_tok = sem("tokens_done")
        s_pad = sem("s_pad")
        s_wtr = sem("s_wtr")
        s_wmean = sem("s_wmean")
        s_wscaled = sem("s_wscaled")
        s_shares = sem("s_shares")
        s_wt = sem("s_wt")
        s_lnc = sem("s_lnc")
        s_x = [sem(f"s_x{i}") for i in range(XR)]
        conv_done = sem("conv_done")
        sq_done = sem("sq_done")
        ssum_done = sem("ssum_done")
        varv_done = sem("varv_done")
        rstd_done = sem("rstd_done")
        xh_done = sem("xh_done")
        tr_done = sem("tr_done")
        act_done = sem("act_done")
        s_tw = sem("s_tw")
        t = {k: sem("t_" + k) for k in
             "h6c h6r st1 mv1 ve1 rs1 xh1 xhT a1 pj x1 st2 mv2 ve2 rs2 xn2 xn2T a2 qkv qk sc msk mx sub ex den rden pT pTc "
             "pv oo ooT a3 at x2 st3 mv3 ve3 rs3 xn3 xn3T a4 lo lg mxl subl exl suml pmax cand first hot coef fin".split()}
        s_w2 = sem("second_weights_here")
        s_b2 = sem("second_biases_here")
        s_w1c = sem("common_weights_here")
        s_zeros = sem("zeros_made")
        s_cleared = sem("rows_cleared")
        s_consts = sem("routing_constants")
        c_up = sem("common_up_done")
        c_act = sem("common_hidden_done")
        c_out = sem("common_down_done")
        c_kept = sem("common_kept")
        c_acc = sem("common_added")
        s_rt = sem("routing_steps")
        s_exl = sem("routing_exponentials")
        s_hot = sem("chosen_known")
        s_rank = sem("ranks_known")
        s_slot = sem("slots_known")
        s_own = sem("owners_known")
        s_sent = sem("tokens_sorted")
        s_w1 = [sem(f"first_weights_here{k}") for k in range(WR)]
        s_xs = [sem(f"tile_tokens_here{k}") for k in range(2)]
        e_turn = sem("tile_turned")
        e_copy = sem("tile_copied")
        e_up = sem("tile_up_done")
        e_act = sem("tile_hidden_done")
        e_down = sem("tile_down_done")
        e_res = sem("tile_result_here")
        s_ys = [sem(f"tile_stored{k}") for k in range(2)]
        s_got = sem("results_gathered")
        s_fin = sem("sum_done")
        s_out = sem("s_out")

        block = ctx.enter_context(nc.Block())

        WEIGHTS = [(projw[:, :], a["L0_tok_proj_w"]), (projb[:, :], a["L0_tok_proj_b"].rearrange("(a c) -> a c", a=1))]
        for src, dst in ((a["L0_attn_w_qkv"], wqkv), (a["L0_attn_w_proj"], wprj), (a["L0_ffn_Ws"], wsr)):
            WEIGHTS += [(dst[:, 0, :], src[0:P, :]), (dst[0:D1, 1, :], src[P:D, :])]
        WEIGHTS.append((wsr[D1:D1 + 1, 1, :], a["L0_ffn_bs"].rearrange("(a c) -> a c", a=1)))

        def shifted(off, cols):
            return bass.AP(xparts.tensor, off, [[BATCH * SAMPLES, 4], [1, K0], [1, cols]])

        def tiles_of(rows, b):
            lo, hi = XBLOCKS[b]
            return rows[lo * BT * SAMPLES:hi * BT * SAMPLES].rearrange("(p c) -> p c", p=P)

        w1_dram, b1_dram = a["L0_ffn_W1"], a["L0_ffn_b1"]

        @block.sync
        def _(sp):
            xin = a["x"].rearrange("b s -> (b s)")
            for b, (lo, hi) in enumerate(XBLOCKS):
                sp.dma_start(xraw[:, lo * XPP:hi * XPP], tiles_of(xin, b)).then_inc(s_xraw[b], 16)
                if b == 0:
                    sp.dma_start(w0raw[:, :, :], a["L0_tok_conv_w0"].rearrange("o i k -> o (i k)").unsqueeze(1)
                                 .to_broadcast([P, 4, K0])).then_inc(s_w0raw, 16)

            def load_x(i, g, read_by, short=False):
                _, start, per, count = G0[g]
                cols = 5 * per * count - (9 if short else 0)
                if read_by is not None:
                    sp.wait_ge(conv_done, read_by + 1)
                sp.dma_start(xr[g % XR][:, 0:cols].bitcast(F32), shifted(i * (BT * SAMPLES) + 5 * start, cols))\
                    .then_inc(s_x[g % XR], 16)

            def store_parts(b):
                lo, hi = XBLOCKS[b]
                sp.wait_ge(s_parts, b + 1)
                for j in range(4):
                    sp.dma_start(tiles_of(xparts[j], b), (xhi, xlo)[j % 2][:, lo * XPP:hi * XPP]).then_inc(s_stored[b], 16)

            body_at = [ORDER.index(0)]
            while len(body_at) < len(G0):
                body_at.append(ORDER.index(0, body_at[-1] + 1))
            head_at = [n for n, s in enumerate(HEAD) if s[1][0] == 0]
            store_parts(0)
            sp.wait_ge(s_stored[0], 64)
            for n in range(2 * len(G0)):
                i, g = n // len(G0), n % len(G0)
                if g == len(G0) - 1:
                    sp.wait_ge(s_stored[i + 1], 64)
                load_x(i, g, head_at[n - XR] if n >= XR else None)
                if n == XR - 1:
                    store_parts(1)
                    for l in range(1, 7):
                        k = CONVS[l][0]
                        sp.dma_start(wraw[:, TAP0[l]:TAP0[l] + k, :].rearrange("p t c -> p (t c)"),
                                     a[f"L0_tok_conv_w{l}"].rearrange("o i k -> o (i k)")).then_inc(s_w, 16)
                if n == len(G0) + XR:
                    store_parts(2)
                if XR < n <= XR + len(WEIGHTS):
                    dst, src = WEIGHTS[n - XR - 1]
                    sp.dma_start(dst, src).then_inc(s_tw, 16)
            for g in range(XR):
                load_x(2, g, head_at[2 * len(G0) + g - XR])

            def later(i, last):
                step = NHD + (i - 2) * NB
                for g in range(XR, len(G0)):
                    load_x(i, g, step + body_at[g - XR], short=last and g == len(G0) - 1)
                if not last:
                    for g in range(XR):
                        load_x(i + 1, g, step + body_at[len(G0) + g - XR])

            with sp.Fori(2, NT - 1) as i:
                later(i, False)
            later(NT - 1, True)

            sp.wait_ge(act_done, NG)
            sp.dma_start(b2s, a["L0_ffn_b2"].rearrange("e d -> (e d)").rearrange("(a c) -> a c", a=1)).then_inc(s_b2, 16)
            sp.wait_ge(s_own, 1)

            def load_weights(j, b, first):
                own = sp.value_load(owni[0:1, bass.ds(j, 1)], min_val=0, max_val=NE - 1)
                if not first:
                    sp.wait_ge(e_up, j - WR + 1)
                sp.dma_start(W1r[:, b, :], w1_dram[bass.ds(own, 1), 0:P, :].rearrange("e p n -> p (e n)")).then_inc(s_w1[b], 16)
                sp.dma_start(W1rb[0:D1, b, :], w1_dram[bass.ds(own, 1), P:D, :].rearrange("e p n -> p (e n)")).then_inc(s_w1[b], 16)
                sp.dma_start(W1rb[D1:D1 + 1, b, :], b1_dram[bass.ds(own, 1), :]).then_inc(s_w1[b], 16)

            def load_tokens(j, b, first):
                if not first:
                    sp.wait_ge(e_turn, j - 1)
                sp.dma_start(xs[:, b, :], xs_dram[bass.ds(j * P, P), :]).then_inc(s_xs[b], 16)

            for j in range(2):
                load_weights(j, j, True)
            sp.wait_ge(s_sent, 16 * NT)
            for j in range(2):
                load_tokens(j, j, True)
            with sp.Fori(0, (NTILE - 3) // 2) as k:
                for b in range(2):
                    load_tokens(2 * k + b + 2, b, False)
                    load_weights(2 * k + b + 2, b, False)
            load_tokens(NTILE - 1, (NTILE - 1) % 2, False)
            load_weights(NTILE - 1, (NTILE - 1) % 2, False)
            sp.wait_ge(s_fin, 1)
            sp.dma_start(out.rearrange("(i b) t d -> (b t) i d", i=NT), acc[:, :, :]).then_inc(s_out, 16)
            sp.wait_ge(s_out, 16)

        @block.gpsimd
        def _(gp):
            gp.memset(ident[:, :], 0.0).then_inc(s_ident, 1)
            gp.wait_ge(s_ident, 1)
            gp.affine_select(out=ident[:, :], in_=ident[:, :], compare_op=ALU.not_equal, fill=1.0,
                             base=0, pattern=[[-1, P]], channel_multiplier=1).then_inc(s_ident, 1)
            gp.memset(w0m[:, :], 1.0).then_inc(s_w0m, 1)
            gp.wait_ge(s_w0m, 1)
            gp.affine_select(out=w0m[:, 0:1], in_=w0m[:, 0:1], compare_op=ALU.is_ge, fill=0.0,
                             base=2 * K0 - 1, pattern=[[0, 1]], channel_multiplier=-1).then_inc(s_w0m, 1)
            gp.affine_select(out=w0m[:, 1:2], in_=w0m[:, 1:2], compare_op=ALU.is_ge, fill=0.0,
                             base=-2 * K0, pattern=[[0, 1]], channel_multiplier=1).then_inc(s_w0m, 2)
            gp.memset(neghalf[:, :], -0.5).then_inc(s_const, 1)
            gp.memset(eps[:, :], EPS).then_inc(s_const, 1)
            gp.memset(ceps[:, :], C * EPS).then_inc(s_const, 1)
            gp.wait_ge(s_const, 3)

            def group(n, idx, g):
                _, _, per, count = g
                gp.wait_ge(ssum_done, n + 1)
                gp.tensor_tensor(varv[0:per, idx, 0:count], ssum[0:per, idx, 0:count], ceps[0:per, 0:count],
                                 ALU.add).then_inc(varv_done, 1)
                gp.wait_ge(varv_done, n + 1)
                gp.tensor_tensor(rstd[0:per, idx, 0:count], varv[0:per, idx, 0:count],
                                 neghalf[0:per, 0:count], ALU.pow).then_inc(rstd_done, 1)

            def power(tag, r):
                gp.wait_ge(t["mv" + tag], r + 1)
                gp.tensor_tensor(veps[:, :], mv[:, 1:2], eps[0:M, :], ALU.add).then_inc(t["ve" + tag], 1)
                gp.wait_ge(t["ve" + tag], r + 1)
                gp.tensor_tensor(rs[:, :], veps[:, :], neghalf[0:M, 0:1], ALU.pow).then_inc(t["rs" + tag], 1)

            def tokens(step, r):
                for name, tag in (("power_h", "1"), ("power_1", "2"), ("power_2", "3")):
                    if step == name:
                        power(tag, r)

            for n, (_, g) in enumerate(HEAD):
                group(n, n % 4, g)
            gp.memset(mask[:, :], 0.0).then_inc(s_const, 1)
            gp.wait_ge(s_const, 4)
            mv3 = mask[:, :].rearrange("p (j c) -> p j c", c=TOK)
            gp.affine_select(out=mv3, in_=mv3, compare_op=ALU.is_ge, fill=-1e30,
                             base=0, pattern=[[-TOK, BT], [0, TOK]], channel_multiplier=1).then_inc(s_const, 1)
            gp.wait_ge(s_const, 5)
            gp.affine_select(out=mv3, in_=mv3, compare_op=ALU.is_ge, fill=-1e30,
                             base=TOK - 1, pattern=[[TOK, BT], [0, TOK]], channel_multiplier=-1).then_inc(s_const, 1)
            gp.iota(iota[:, :], pattern=[[1, NE]], base=0, channel_multiplier=0,
                    allow_small_or_imprecise_dtypes=True).then_inc(s_const, 1)

            gp.memset(zero[:, :], 0.0).then_inc(s_zeros, 1)
            gp.wait_ge(s_zeros, 1)
            gp.dma_start(xs_dram[0:NTILE * P, :].rearrange("(j p) d -> p j d", p=P),
                         zero[:, :].unsqueeze(1).to_broadcast([P, NTILE, D])).then_inc(s_cleared, 16)
            gp.dma_start(ys_dram[NTILE * P:ROWS, :].rearrange("(j p) d -> p j d", p=P),
                         zero[:, :].unsqueeze(1).to_broadcast([P, TOKENS // P, D])).then_inc(s_cleared, 16)
            gp.memset(upper[:, :], 1.0).then_inc(s_consts, 1)
            gp.memset(onesm[:, :], 1.0).then_inc(s_consts, 1)
            gp.memset(below[:, :, :], 1.0).then_inc(s_consts, 1)
            gp.memset(dump[:, :], 0.0).then_inc(s_consts, 1)
            gp.wait_ge(s_consts, 4)
            gp.affine_select(out=upper[:, :], in_=upper[:, :], compare_op=ALU.is_gt, fill=0.0,
                             base=0, pattern=[[1, M]], channel_multiplier=-1).then_inc(s_consts, 1)
            gp.affine_select(out=below[:, :, :], in_=below[:, :, :], compare_op=ALU.is_gt, fill=0.0,
                             base=0, pattern=[[1, NE], [-1, NE]], channel_multiplier=0).then_inc(s_consts, 1)
            gp.wait_ge(s_consts, 6)
            gp.memset(below[:, :, 0:1], 0.0).then_inc(s_consts, 1)
            gp.memset(dump[:, 0:1], float(NTILE)).then_inc(s_consts, 1)
            gp.iota(full[:, :, :], pattern=[[0, NE], [P, TOKENS // P]], base=0, channel_multiplier=0,
                    allow_small_or_imprecise_dtypes=True).then_inc(s_consts, 1)
            gp.iota(jota[:, :, :], pattern=[[1, NTILE], [0, NE]], base=0, channel_multiplier=0,
                    allow_small_or_imprecise_dtypes=True).then_inc(s_consts, 1)
            with gp.Fori(2, NT) as i:
                for k, (_, g) in enumerate(BODY):
                    group(NHD + (i - 2) * NB + k, (NHD + k) % 4, g)
                    for step in AT[k]:
                        tokens(step, i - 2)
            for k, steps in enumerate(LAST_STEPS):
                if k < NE_SLOTS and ENDING[LAG + k] is not None:
                    n = ENDING[LAG + k]
                    group(n, n % 4, ALL[n][1])
                for step, run in steps:
                    tokens(step, run)

            gp.wait_ge(s_cleared, 32)
            gp.wait_ge(s_slot, 1)
            for i in range(NT):
                gp.indirect_dma_start(out=xs_dram[:, :], out_offset=bass.IndirectOffsetOnAxis(ap=sloti[:, i:i + 1], axis=0),
                                      in_=xn3[:, i, :], in_offset=None).then_inc(s_sent, 16)
            for b in range(2):
                gp.wait_ge(s_ys[b], 16 * ((NTILE - b + 1) // 2))
            for i in range(NT):
                gp.indirect_dma_start(out=sel[:, i, :], out_offset=None, in_=ys_dram[:, :],
                                      in_offset=bass.IndirectOffsetOnAxis(ap=sloti[:, i:i + 1], axis=0)).then_inc(s_got, 16)

        @block.tensor
        def _(pe):
            pe.wait_ge(s_ident, 2)
            pe.wait_ge(s_w0raw, 16)
            nc.tensor.transpose(ps[0:4 * K0, 4, 0:C], w0raw[:, :, :].rearrange("p j k -> p (j k)"), ident[:, :]).then_inc(s_wtr, 1)
            pe.wait_ge(s_w0t, 1)

            def turn_taps(q):
                if q == 0:
                    pe.wait_ge(s_w, 16 * 6)
                if q >= 2:
                    pe.wait_ge(s_wt, q)
                for j in range(4):
                    l, tap = W_TAPS[4 * q + j]
                    k = CONVS[l][0]
                    src = wraw[:, TAP0[l]:TAP0[l] + k, :].rearrange("p t c -> p (t c)")\
                        .rearrange("p (c t) -> p t c", t=k)[:, tap, :]
                    last = nc.tensor.transpose(ps[:, 6 + q % 2, j * C:(j + 1) * C], src, ident[:, :])
                last.then_inc(s_wtr, 1)

            def conv(n, idx, g, tile, feed, early):
                layer, start, per, count = g
                if not early:
                    pe.wait_ge(xh_done, n - YBUF + 1)
                if layer == 0:
                    gi = G0.index(g)
                    pe.wait_ge(s_x[gi % XR], xwait(tile, gi))
                    for j in range(count):
                        last = nc.tensor.matmul(y[idx][0:per, j * C:(j + 1) * C],
                                                xr[gi % XR][:, 5 * per * j:5 * per * (j + 1):5], w0t[:, :],
                                                start=True, stop=True)
                    last.then_inc(conv_done, 1)
                    return
                pe.wait_ge(act_done, feed + 1)
                taps, st = CONVS[layer]
                for j in range(count):
                    for tap in range(taps):
                        lo = st * (start + per * j) + tap
                        src = h[layer - 1][:, lo:lo + st * (per - 1) + 1:st]
                        last = nc.tensor.matmul(y[idx][0:per, j * C:(j + 1) * C], src, wt[:, TAP0[layer] + tap, :],
                                                start=(tap == 0), stop=(tap == taps - 1))
                last.then_inc(conv_done, 1)

            def xwait(i, gi):
                return (i * (len(G0) // XR) + gi // XR + 1) * 16

            def turn(n, idx, g, early):
                _, _, per, count = g
                pe.wait_ge(xh_done, n + 1)
                if not early:
                    pe.wait_ge(act_done, n - TRBUF + 1)
                for j in range(count):
                    last = nc.tensor.transpose(tr[idx % TRBUF][:, j * per:(j + 1) * per],
                                               xh[0:per, idx % XHBUF, j * C:(j + 1) * C], ident[0:per, 0:per])
                last.then_inc(tr_done, 1)

            def turn2(src, ready, done, r):
                pe.wait_ge(ready, r + 1)
                nc.tensor.transpose(pb[:, 0:M], src[:, 0:P], ident[0:M, 0:M])
                nc.tensor.transpose(pb[0:D1, M:2 * M], src[:, P:D], ident[0:M, 0:M]).then_inc(done, 1)

            def tokens(step, r, h6_ready):
                if step == "turn_h":
                    pe.wait_ge(act_done, h6_ready)
                    nc.tensor.transpose(pa[0:M, 0:C], h6[:, :], ident[:, :]).then_inc(t["h6r"], 1)
                if step == "turn_norm_h":
                    pe.wait_ge(t["xh1"], r + 1)
                    nc.tensor.transpose(pb[:, 0:M], xn[:, 0:C], ident[0:M, 0:M]).then_inc(t["xhT"], 1)
                if step == "project":
                    pe.wait_ge(t["a1"], r + 1)
                    nc.tensor.matmul(pa[0:M, 0:D], act[:, 0, :], projw[:, :], start=True, stop=False)
                    nc.tensor.matmul(pa[0:M, 0:D], ones[0:1, 0:M], projb[0:1, :], start=False, stop=True).then_inc(t["pj"], 1)
                if step == "turn_1":
                    turn2(xn, t["xn2"], t["xn2T"], r)
                if step == "qkv":
                    pe.wait_ge(t["a2"], r + 1)
                    for j in range(4):
                        lo = (j // 2) * D + (j % 2) * P
                        w = D1 if j % 2 else P
                        o = pa[0:w, j * M:(j + 1) * M]
                        nc.tensor.matmul(o, wqkv[:, 0, lo:lo + w], act[:, 0, :], start=True, stop=False)
                        nc.tensor.matmul(o, wqkv[0:D1, 1, lo:lo + w], act[0:D1, 1, :], start=False, stop=True)
                    nc.tensor.matmul(pb[0:M, 0:D], act[:, 0, :], wqkv[:, 0, 2 * D:3 * D], start=True, stop=False)
                    nc.tensor.matmul(pb[0:M, 0:D], act[0:D1, 1, :], wqkv[0:D1, 1, 2 * D:3 * D], start=False, stop=True)\
                        .then_inc(t["qkv"], 1)
                if step == "scores":
                    pe.wait_ge(t["qk"], r + 1)
                    for hd in range(NH):
                        rows = P if hd < 4 else D1
                        last = nc.tensor.matmul((pa, pb)[hd // 3][0:M, (hd % 3) * M:(hd % 3 + 1) * M], qm[0:rows, hd, :],
                                                kT[0:rows, hd // 4, :], start=True, stop=True)
                    last.then_inc(t["sc"], 1)
                if step == "turn_probs":
                    pe.wait_ge(t["ex"], r + 1)
                    for hd in range(NH):
                        last = nc.tensor.transpose((pa, pb)[hd // 3][0:M, (hd % 3) * M:(hd % 3 + 1) * M], t1[:, hd, :],
                                                   ident[0:M, 0:M])
                    last.then_inc(t["pT"], 1)
                if step == "values":
                    pe.wait_ge(t["pTc"], r + 1)
                    for hd in range(NH):
                        last = nc.tensor.matmul(pa[0:M, hd * HD:(hd + 1) * HD], pT[:, hd, :], vv[:, hd * HD:(hd + 1) * HD],
                                                start=True, stop=True)
                    last.then_inc(t["pv"], 1)
                if step == "turn_heads":
                    turn2(oo, t["oo"], t["ooT"], r)
                if step == "out_project":
                    pe.wait_ge(t["a3"], r + 1)
                    nc.tensor.matmul(pa[0:M, 0:D], act[:, 0, :], wprj[:, 0, :], start=True, stop=False)
                    nc.tensor.matmul(pa[0:M, 0:D], act[0:D1, 1, :], wprj[0:D1, 1, :], start=False, stop=True).then_inc(t["at"], 1)
                if step == "turn_2":
                    turn2(xn, t["xn3"], t["xn3T"], r)
                if step == "logits":
                    pe.wait_ge(t["a4"], r + 1)
                    nc.tensor.matmul(pb[0:M, 0:NE], act[:, 0, :], wsr[:, 0, :], start=True, stop=False)
                    nc.tensor.matmul(pb[0:M, 0:NE], act[0:D1 + 1, 1, :], wsr[0:D1 + 1, 1, :], start=False, stop=True)\
                        .then_inc(t["lo"], 1)

            def common_up(half, f):
                u = half * NF + f
                if u == 0:
                    pe.wait_ge(s_w1c, 16 * 4)
                    pe.wait_ge(s_w2, 16 * NE)
                if u >= 4:
                    pe.wait_ge(c_act, u - 3)
                if u == NF + 2:
                    pe.wait_ge(c_kept, HALF)
                o = ps[:, u % 4, 0:HALF * M]
                cols = slice(half * HALF * M, (half + 1) * HALF * M)
                nc.tensor.matmul(o, W1c[:, f * P:(f + 1) * P], xt[:, cols], start=True, stop=False)
                nc.tensor.matmul(o, W1cb[:, f * P:(f + 1) * P], xtb[:, cols], start=False, stop=True).then_inc(c_up, 1)

            def common_down(i):
                if i % HALF == 0:
                    pe.wait_ge(c_act, NF * (i // HALF + 1))
                o = ps[0:M, COMMON_BANK[i], 0:D]
                for f in range(NF):
                    nc.tensor.matmul(o, hc[:, f, i * M:(i + 1) * M], W2s[:, 0, f, :], start=(f == 0), stop=False)
                nc.tensor.matmul(o, ones[0:1, 0:M], b2c[0:1, :], start=False, stop=True).then_inc(c_out, 1)

            for n, (tile, g) in enumerate(HEAD):
                conv(n, n % 4, g, tile, last_feed(n), n < YBUF)
                if n == LAG - 1:
                    pe.wait_ge(s_ln, 16 * 16)
                    nc.tensor.transpose(ps[:, 5, 0:16], lnraw[:, :], ident[0:16, 0:16]).then_inc(s_wtr, 1)
                if n == LAG:
                    pe.wait_ge(s_lnc, 1)
                if n >= LAG:
                    turn(n - LAG, (n - LAG) % 4, HEAD[n - LAG][1], n - LAG < TRBUF)
                if n in TAPS_AT:
                    turn_taps(TAPS_AT.index(n))
                if n == len(G0) - 1:
                    pe.wait_ge(s_wt, 1 + NTAP // 4)
                    pe.wait_ge(s_pad, 4)
            pe.wait_ge(s_tw, 16 * 9)
            pe.wait_ge(s_pad, 10)
            with pe.Fori(2, NT) as i:
                for k, (d, g) in enumerate(BODY):
                    n = NHD + (i - 2) * NB + k
                    conv(n, (NHD + k) % 4, g, i - d, None if BACK[k] is None else n - BACK[k], False)
                    turn(n - LAG, (NHD + k - LAG) % 4, BODY[k - LAG][1], False)
                    if k == 0:
                        pe.wait_ge(s_tok, i - 1)
                    for step in AT[k]:
                        tokens(step, i - 2, n - H6_BACK + 1 if k == 0 else None)
            for k, steps in enumerate(LAST_STEPS):
                if k < NE_SLOTS:
                    now, before = ENDING[LAG + k], ENDING[k]
                    if now is not None:
                        conv(now, now % 4, ALL[now][1], NT, last_feed(now), False)
                    if before is not None:
                        turn(before, before % 4, ALL[before][1], False)
                for step, run in steps:
                    if step == STEPS[0]:
                        pe.wait_ge(s_tok, run + 1)
                    tokens(step, run, ALL.index((run - 1, G6[0])) + 1)
                if k in COMMON_AT:
                    item = COMMON_AT.index(k)
                    if item < NF:
                        common_up(0, item)
                    else:
                        common_down(item - NF)
            pe.wait_ge(s_tok, NT + 2)

            common_up(1, 0)
            common_up(1, 1)
            pe.wait_ge(s_consts, 10)
            pe.wait_ge(s_hot, 1)
            rank = pa[0:M, 0:NT * NE]
            flat = hot[:, :, :].rearrange("p i e -> p (i e)")
            nc.tensor.matmul(rank, upper[:, :], flat, start=True, stop=False)
            for d in range(1, NT):
                nc.tensor.matmul(pa[0:M, d * NE:NT * NE], onesm[:, :], flat[:, 0:(NT - d) * NE], start=False, stop=(d == NT - 1))
            for i in range(NT):
                last = nc.tensor.matmul(pb[0:M, 0:NE], onesm[:, :], hot[:, i, :], start=(i == 0), stop=(i == NT - 1))
            last.then_inc(s_rank, 1)
            for f in range(2, NF):
                common_up(1, f)
            for i in range(HALF, NT):
                common_down(i)

            def turn_tile(j, half, b):
                pe.wait_ge(s_xs[b], 16 * (half + 1))
                if isinstance(j, int) and j == 0:
                    pe.wait_ge(s_hot, 1)
                else:
                    pe.wait_ge(e_copy, j)
                nc.tensor.transpose(pb[:, 0:P], xs[:, b, 0:P], ident[:, :])
                nc.tensor.transpose(pb[0:D1, P:2 * P], xs[:, b, P:D], ident[:, :]).then_inc(e_turn, 1)

            def up(j, half, b, first=False):
                pe.wait_ge(e_copy, j + 1)
                pe.wait_ge(s_w1[b], 48 * (half + 1))
                if not first:
                    pe.wait_ge(e_act, j - 1)
                for f in range(NF):
                    o = ps[:, 2 * b + f // 4, (f % 4) * P:(f % 4 + 1) * P]
                    nc.tensor.matmul(o, W1r[:, b, f * P:(f + 1) * P], xst[:, b, :], start=True, stop=False)
                    last = nc.tensor.matmul(o, W1rb[:, b, f * P:(f + 1) * P], xstb[:, b, :], start=False, stop=True)
                last.then_inc(e_up, 1)

            def down(j, b, first=False):
                own = pe.value_load(owni[0:1, bass.ds(j, 1)], min_val=0, max_val=NE - 1)
                pe.wait_ge(e_act, j + 1)
                if not first:
                    pe.wait_ge(e_res, j - 1)
                o = ps[:, 4 + b, 0:D]
                for f in range(NF):
                    nc.tensor.matmul(o, ht[:, b, f * P:(f + 1) * P],
                                     W2s[:, bass.ds(own, 1), f, :].rearrange("p e d -> p (e d)"), start=(f == 0), stop=False)
                nc.tensor.matmul(o, ones[0:1, :], b2s[0:1, bass.ds(own * D, D)], start=False, stop=True).then_inc(e_down, 1)

            pe.wait_ge(s_own, 1)
            turn_tile(0, 0, 0)
            pe.wait_ge(s_b2, 16)
            pe.wait_ge(c_acc, NT - HALF)
            turn_tile(1, 0, 1)
            up(0, 0, 0, True)
            turn_tile(2, 1, 0)
            up(1, 0, 1, True)
            down(0, 0, True)
            turn_tile(3, 1, 1)
            up(2, 1, 0)
            down(1, 1, True)
            with pe.Fori(1, (NTILE - 1) // 2 - 1) as k:
                turn_tile(2 * k + 2, k + 1, 0)
                up(2 * k + 1, k, 1)
                down(2 * k, 0)
                turn_tile(2 * k + 3, k + 1, 1)
                up(2 * k + 2, k + 1, 0)
                down(2 * k + 1, 1)
            L = NTILE - 1
            turn_tile(L, L // 2, 0)
            up(L - 1, (L - 1) // 2, 1)
            down(L - 2, 0)
            up(L, L // 2, 0)
            down(L - 1, 1)
            down(L, 0)

        @block.vector
        def _(ve):
            def part(b):
                lo, hi = (t * XPP for t in XBLOCKS[b])
                ve.wait_ge(s_xraw[b], 16)
                nc.vector.tensor_copy(xhi[:, lo:hi].bitcast(F32R), xraw[:, lo:hi]).then_inc(s_high, 1)
                ve.wait_ge(s_high, b + 1)
                nc.vector.tensor_tensor(xlo[:, lo:hi].bitcast(F32R), xraw[:, lo:hi], xhi[:, lo:hi], ALU.subtract)\
                    .then_inc(s_parts, 1)

            def centre(done, dst, src, rows, cnt):
                if done:
                    ve.wait_ge(s_wt, done)
                nc.vector.reduce_sum(wmean[0:rows, 0:cnt], src, axis=X).then_inc(s_wmean, 1)
                ve.wait_ge(s_wmean, done + 1)
                nc.vector.tensor_scalar(wscaled[0:rows, 0:cnt], wmean[0:rows, 0:cnt], 1.0 / C, None,
                                        ALU.mult).then_inc(s_wscaled, 1)
                ve.wait_ge(s_wscaled, done + 1)
                for j in range(cnt):
                    last = nc.vector.tensor_scalar(dst[:, j, :], src[:, j, :], wscaled[0:rows, j:j + 1], None, ALU.subtract)
                last.then_inc(s_wt, 1)

            def centre_taps(q):
                ve.wait_ge(s_wtr, q + 3)
                centre(q + 1, wt[:, 4 * q:4 * q + 4, :], ps[:, 6 + q % 2, :].rearrange("p (t c) -> p t c", c=C), P, 4)

            part(0)
            ve.wait_ge(s_wtr, 1)
            centre(0, w0c[:, :].unsqueeze(1), ps[0:4 * K0, 4, 0:C].unsqueeze(1), 4 * K0, 1)
            ve.wait_ge(s_wt, 1)
            nc.vector.tensor_copy(w0h[:, :], w0c[:, :]).then_inc(s_w0s, 1)
            ve.wait_ge(s_w0s, 1)
            nc.vector.tensor_tensor(w0c[:, :], w0c[:, :], w0h[:, :].bitcast(F32), ALU.subtract).then_inc(s_w0s, 1)
            ve.wait_ge(s_w0s, 2)
            ve.wait_ge(s_w0m, 4)
            nc.vector.tensor_scalar(w0c[:, :], w0c[:, :], w0m[:, 1:2], None, ALU.mult).then_inc(s_w0s, 1)
            ve.wait_ge(s_w0s, 3)
            nc.vector.scalar_tensor_tensor(out=w0t[:, :], in0=w0h[:, :].bitcast(F32), scalar=w0m[:, 0:1], in1=w0c[:, :],
                                           op0=ALU.mult, op1=ALU.add).then_inc(s_w0t, 1)
            part(1)
            for l in range(4):
                nc.vector.memset(h[l][:, FLAT[l]:FLAT[l] + 1], 0.0).then_inc(s_pad, 1)
            nc.vector.memset(ones[:, :], 1.0).then_inc(s_pad, 1)
            nc.vector.memset(h6[:, :], 0.0).then_inc(s_pad, 1)
            nc.vector.memset(xtb_[D1:D1 + 1, :], 1.0).then_inc(s_pad, 1)
            nc.vector.memset(act[D1:D1 + 1, 1, :], 1.0).then_inc(s_pad, 1)
            nc.vector.memset(xstb[D1:D1 + 1, :, :], 1.0).then_inc(s_pad, 1)
            nc.vector.memset(qm[:, :, :], 0.0).then_inc(s_pad, 1)

            def group(n, idx, g, early):
                _, _, per, count = g
                w = count * C
                ve.wait_ge(sq_done, n + 1)
                nc.vector.reduce_sum(ssum[0:per, idx, 0:count],
                                     sq[0:per, idx % SQBUF, 0:w].rearrange("p (j c) -> p j c", c=C), axis=X).then_inc(ssum_done, 1)

            def norm(n, idx, g, early):
                _, _, per, count = g
                w = count * C
                ve.wait_ge(rstd_done, n + 1)
                if not early:
                    ve.wait_ge(tr_done, n - XHBUF + 1)
                nc.vector.tensor_tensor(xh[0:per, idx % XHBUF, 0:w].rearrange("p (j c) -> p j c", c=C),
                                        y[idx][0:per, 0:w].rearrange("p (j c) -> p j c", c=C),
                                        rstd[0:per, idx, 0:count].unsqueeze(2).to_broadcast([per, count, C]),
                                        ALU.mult).then_inc(xh_done, 1)

            def stat(src, tag, wait, r):
                if wait is not None:
                    ve.wait_ge(wait, r + 1)
                nc.vector.bn_stats(stats[:, :], src).then_inc(t["st" + tag], 1)
                ve.wait_ge(s_pad, 10)
                ve.wait_ge(t["st" + tag], r + 1)
                nc.vector.bn_aggr(mv[:, :], stats[:, :]).then_inc(t["mv" + tag], 1)

            def normed(dst, src, tag, done, r):
                ve.wait_ge(t["rs" + tag], r + 1)
                nc.vector.tensor_scalar(dst, src, mv[:, 0:1], rs[:, 0:1], ALU.subtract, ALU.mult).then_inc(done, 1)

            def tokens(step, r):
                if step == "stat_h":
                    stat(pa[0:M, 0:C], "1", t["h6r"], r)
                if step == "norm_h":
                    normed(xn[:, 0:C], pa[0:M, 0:C], "1", t["xh1"], r)
                if step == "stat_1":
                    ve.wait_ge(t["pj"], r + 1)
                    nc.vector.tensor_copy(x1[:, :], pa[0:M, 0:D]).then_inc(t["x1"], 1)
                    stat(x1[:, :], "2", t["x1"], r)
                if step == "norm_1":
                    normed(xn[:, :], x1[:, :], "2", t["xn2"], r)
                if step == "split_heads":
                    ve.wait_ge(t["qkv"], r + 1)
                    for hd in range(NH):
                        lo = (hd % 4) * HD
                        nc.vector.tensor_copy(qm[lo:lo + HD, hd, :], pa[lo:lo + HD, (hd // 4) * M:(hd // 4 + 1) * M])
                    nc.vector.tensor_copy(kT[:, 0, :], pa[:, 2 * M:3 * M])
                    nc.vector.tensor_copy(kT[0:D1, 1, :], pa[0:D1, 3 * M:4 * M])
                    nc.vector.tensor_copy(vv[:, :], pb[0:M, 0:D]).then_inc(t["qk"], 1)
                if step == "mask":
                    ve.wait_ge(t["sc"], r + 1)
                    for half in range(2):
                        last = nc.vector.tensor_tensor(t1[:, 3 * half:3 * half + 3, :],
                                                       (pa, pb)[half][0:M, 0:3 * M].rearrange("p (h k) -> p h k", h=3),
                                                       mask[:, :].unsqueeze(1).to_broadcast([M, 3, M]), ALU.add)
                    last.then_inc(t["msk"], 1)
                    ve.wait_ge(t["msk"], r + 1)
                    nc.vector.reduce_max(mx[:, :], t1[:, :, :], axis=X).then_inc(t["mx"], 1)
                if step == "less_max":
                    ve.wait_ge(t["mx"], r + 1)
                    nc.vector.tensor_tensor(t1[:, :, :], t1[:, :, :], mx[:, :].unsqueeze(2).to_broadcast([M, NH, M]),
                                            ALU.subtract).then_inc(t["sub"], 1)
                if step == "turn_probs":
                    ve.wait_ge(t["ex"], r + 1)
                    nc.vector.reduce_sum(den[:, :], t1[:, :, :], axis=X).then_inc(t["den"], 1)
                    ve.wait_ge(t["den"], r + 1)
                    nc.vector.reciprocal(rden[:, :], den[:, :]).then_inc(t["rden"], 1)
                if step == "copy_probs":
                    ve.wait_ge(t["pT"], r + 1)
                    for half in range(2):
                        last = nc.vector.tensor_copy(pT[:, 3 * half:3 * half + 3, :],
                                                     (pa, pb)[half][0:M, 0:3 * M].rearrange("p (h k) -> p h k", h=3))
                    last.then_inc(t["pTc"], 1)
                if step == "divide":
                    ve.wait_ge(t["rden"], r + 1)
                    ve.wait_ge(t["pv"], r + 1)
                    nc.vector.tensor_tensor(oo[:, :].rearrange("p (h d) -> p h d", h=NH),
                                            pa[0:M, 0:D].rearrange("p (h d) -> p h d", h=NH),
                                            rden[:, :].unsqueeze(2).to_broadcast([M, NH, HD]), ALU.mult).then_inc(t["oo"], 1)
                if step == "residual":
                    ve.wait_ge(t["at"], r + 1)
                    nc.vector.tensor_tensor(x1[:, :], pa[0:M, 0:D], x1[:, :], ALU.add).then_inc(t["x2"], 1)
                    ve.wait_ge(t["x2"], r + 1)
                    nc.vector.tensor_copy(acc_[:, bass.ds(r, 1), :], x1[:, :].unsqueeze(1))
                    stat(x1[:, :], "3", None, r)
                if step == "norm_2":
                    normed(xn[:, :], x1[:, :], "3", t["xn3"], r)
                    nc.vector.tensor_scalar(xn3_[:, bass.ds(r, 1), :], x1[:, :].unsqueeze(1), mv[:, 0:1], rs[:, 0:1],
                                            ALU.subtract, ALU.mult)
                if step == "keep_logits":
                    ve.wait_ge(t["lo"], r + 1)
                    nc.vector.tensor_copy(lga_[:, bass.ds(r, 1), :], pb[0:M, 0:NE].unsqueeze(1)).then_inc(s_tok, 1)

            nc.vector.memset(r0[:, :], 0.0).then_inc(s_tok, 1)
            for n, (_, g) in enumerate(HEAD):
                group(n, n % 4, g, n < XHBUF)
                if n >= 1:
                    norm(n - 1, (n - 1) % 4, HEAD[n - 1][1], n - 1 < XHBUF)
                if n == LAG - 1:
                    ve.wait_ge(s_wtr, 2)
                    nc.vector.tensor_copy(lncol[:, 7:16], ps[:, 5, 7:16])
                    nc.vector.tensor_scalar(lncol[:, 0:7], ps[:, 5, 0:7], float(C) ** 0.5, None, ALU.mult).then_inc(s_lnc, 1)
                if n in TAPS_AT:
                    centre_taps(TAPS_AT.index(n))
                if n == len(G0):
                    part(2)
            ve.wait_ge(s_const, 7)
            with ve.Fori(2, NT) as i:
                for k, (_, g) in enumerate(BODY):
                    n = NHD + (i - 2) * NB + k
                    group(n, (NHD + k) % 4, g, False)
                    norm(n - 1, (NHD + k - 1) % 4, BODY[k - 1][1], False)
                    for step in AT[k]:
                        tokens(step, i - 2)
            for k, steps in enumerate(LAST_STEPS):
                if k < NE_SLOTS:
                    now, before = ENDING[LAG + k], ENDING[LAG - 1 + k]
                    if now is not None:
                        group(now, now % 4, ALL[now][1], False)
                    if before is not None:
                        norm(before, before % 4, ALL[before][1], False)
                for step, run in steps:
                    tokens(step, run)
                if k - 1 in COMMON_AT[NF:]:
                    item = COMMON_AT.index(k - 1) - NF
                    ve.wait_ge(c_out, item + 1)
                    nc.vector.tensor_copy(kept[:, item, :], ps[0:M, COMMON_BANK[item], 0:D]).then_inc(c_kept, 1)

            step = [0]

            def chain(ins):
                step[0] += 1
                ins.then_inc(s_rt, 1)
                ve.wait_ge(s_rt, step[0])

            def over(x, n=NE):
                return x.unsqueeze(2).to_broadcast([M, NT, n])

            ve.wait_ge(s_tok, NT + 2)
            ve.wait_ge(s_consts, 10)
            chain(nc.vector.reduce_max(r8[:, 0, :], lga[:, :, :], axis=X))
            chain(nc.vector.tensor_tensor(lgb[:, :, :], lga[:, :, :], over(r8[:, 0, :]), ALU.subtract))
            chain(nc.vector.tensor_scalar(lga[:, :, :], lgb[:, :, :], 0.0, 100.0, ALU.is_lt, ALU.mult))
            ioe = iota[:, :].unsqueeze(1).to_broadcast([M, NT, NE])
            chain(nc.vector.tensor_tensor(lga[:, :, :], lga[:, :, :], ioe, ALU.add))
            chain(nc.vector.tensor_reduce(r8[:, 1, :], lga[:, :, :], axis=X, op=ALU.min))
            nc.vector.tensor_tensor(hot[:, :, :], ioe, over(r8[:, 1, :]), ALU.is_equal).then_inc(s_hot, 1)
            ve.wait_ge(s_exl, 1)
            chain(nc.vector.reduce_sum(r8[:, 2, :], lgb[:, :, :], axis=X))
            chain(nc.vector.reciprocal(r8[:, 3, :], r8[:, 2, :]))
            chain(nc.vector.tensor_scalar(r8[:, 4, :], r8[:, 3, :], -1.0, 1.0, ALU.mult, ALU.add))
            chain(nc.vector.tensor_tensor(r8[:, 5, :], r8[:, 3, :], r8[:, 2, :], ALU.mult))
            chain(nc.vector.tensor_tensor(r8[:, 6, :], r8[:, 5, :], r8[:, 4, :], ALU.subtract))
            ve.wait_ge(s_hot, 1)
            chain(nc.vector.tensor_tensor(r8[:, 7, :], r8[:, 6, :], hot[:, :, 0], ALU.mult))
            chain(nc.vector.tensor_tensor(c0[:, :], r8[:, 7, :], r8[:, 4, :], ALU.add))
            ve.wait_ge(s_rank, 1)
            chain(nc.vector.tensor_tensor(tiles3[:, :, :], pb[0:M, 0:NE].unsqueeze(2).to_broadcast([M, NE, TOKENS // P]),
                                          full[:, :, :], ALU.is_gt))
            chain(nc.vector.reduce_sum(tiles[:, :], tiles3[:, :, :], axis=X))
            chain(nc.vector.tensor_tensor(base3[:, :, :], below[:, :, :], tiles[:, :].unsqueeze(1).to_broadcast([M, NE, NE]), ALU.mult))
            chain(nc.vector.reduce_sum(basev[:, :], base3[:, :, :], axis=X))
            chain(nc.vector.tensor_tensor(upto[:, :], basev[0:1, :], tiles[0:1, :], ALU.add))
            chain(nc.vector.tensor_tensor(own3[:, :, 1:NE], upto[:, 1:NE].unsqueeze(1).to_broadcast([1, NTILE, NE - 1]),
                                          jota[:, :, 1:NE], ALU.is_le))
            chain(nc.vector.reduce_sum(ownf[:, :], own3[:, :, 1:NE], axis=X))
            chain(nc.vector.tensor_scalar(ownf[:, :], ownf[:, :], 1.0, float(NE - 1), ALU.add, ALU.min))
            nc.vector.tensor_copy(owni[:, :], ownf[:, :]).then_inc(s_own, 1)
            chain(nc.vector.tensor_tensor(basev[:, :], basev[:, :], dump[:, :], ALU.add))
            chain(nc.vector.tensor_scalar(base2[:, :], basev[:, :], float(P), None, ALU.mult))
            chain(nc.vector.tensor_tensor(lga[:, :, :], pa[0:M, 0:NT * NE].rearrange("p (i e) -> p i e", i=NT),
                                          base2[:, :].unsqueeze(1).to_broadcast([M, NT, NE]), ALU.add))
            chain(nc.vector.tensor_tensor(lga[:, :, :], lga[:, :, :], hot[:, :, :], ALU.mult))
            chain(nc.vector.reduce_sum(slotf[:, :], lga[:, :, :], axis=X))
            nc.vector.tensor_copy(sloti[:, :], slotf[:, :]).then_inc(s_slot, 1)

            for i in [*range(HALF, NT), *range(HALF)]:
                if i >= HALF:
                    ve.wait_ge(c_out, i + 1)
                else:
                    ve.wait_ge(c_kept, i + 1)
                nc.vector.scalar_tensor_tensor(out=acc[:, i, :], in0=ps[0:M, COMMON_BANK[i], 0:D] if i >= HALF else kept[:, i, :],
                                               scalar=c0[:, i:i + 1], in1=acc[:, i, :], op0=ALU.mult, op1=ALU.add).then_inc(c_acc, 1)

            def take(j, b, first=False):
                ve.wait_ge(e_turn, j + 1)
                if not first:
                    ve.wait_ge(e_up, j - 1)
                nc.vector.tensor_copy(xst[:, b, :], pb[:, 0:P])
                nc.vector.tensor_copy(xstb[0:D1, b, :], pb[0:D1, P:2 * P]).then_inc(e_copy, 1)

            def result(j, half, b, first=False):
                ve.wait_ge(e_down, j + 1)
                if not first:
                    ve.wait_ge(s_ys[b], 16 * half)
                nc.vector.tensor_copy(ysb[:, b, :], ps[:, 4 + b, 0:D]).then_inc(e_res, 1)

            take(0, 0, True)
            take(1, 1, True)
            take(2, 0)
            result(0, 0, 0, True)
            take(3, 1)
            result(1, 0, 1, True)
            with ve.Fori(1, (NTILE - 1) // 2 - 1) as k:
                take(2 * k + 2, 0)
                result(2 * k, k, 0)
                take(2 * k + 3, 1)
                result(2 * k + 1, k, 1)
            L = NTILE - 1
            take(L, 0)
            result(L - 2, (L - 2) // 2, 0)
            result(L - 1, (L - 1) // 2, 1)
            result(L, L // 2, 0)
            ve.wait_ge(s_got, 16 * NT)
            ve.wait_ge(c_acc, NT)
            for i in range(NT):
                last = nc.vector.scalar_tensor_tensor(out=acc[:, i, :], in0=sel[:, i, :], scalar=r8[:, 3, i:i + 1],
                                                      in1=acc[:, i, :], op0=ALU.mult, op1=ALU.add)
            last.then_inc(s_fin, 1)

        @block.scalar
        def _(ac):
            for l in range(8):
                layer = f"L0_tok_ln_%s{l}" if l < 7 else "L0_tok_fln_%s"
                ac.dma_start(lnraw[l:l + 1, :], a[layer % "g"].rearrange("(a c) -> a c", a=1)).then_inc(s_ln, 16)
                ac.dma_start(lnraw[8 + l:9 + l, :], a[layer % "b"].rearrange("(a c) -> a c", a=1)).then_inc(s_ln, 16)

            def square(n, idx, g, early):
                _, _, per, count = g
                w = count * C
                ac.wait_ge(conv_done, n + 1)
                if not early:
                    ac.wait_ge(ssum_done, n - SQBUF + 1)
                nc.scalar.activation(sq[0:per, idx % SQBUF, 0:w], y[idx][0:per, 0:w], ACT.Square).then_inc(sq_done, 1)

            def gelu(n, idx, g):
                layer, start, per, count = g
                w = count * per
                ac.wait_ge(tr_done, n + 1)
                src = tr[idx % TRBUF][:, 0:w]
                if layer == 6:
                    dst = h6[:, :]
                elif layer == 5:
                    src = src.rearrange("p (b q) -> p b q", b=BT)[:, :, 0:LAST5]
                    dst = h[5][:, :].rearrange("p (b q) -> p b q", b=BT)
                else:
                    dst = h[layer][:, start:start + w]
                nc.scalar.activation(dst, src, ACT.Gelu, bias=lncol[:, 8 + layer:9 + layer],
                                     scale=lncol[:, layer:layer + 1]).then_inc(act_done, 1)

            def copy2(wait, done, r):
                ac.wait_ge(wait, r + 1)
                nc.scalar.copy(act[:, 0, :], pb[:, 0:M])
                nc.scalar.copy(act[0:D1, 1, :], pb[0:D1, M:2 * M]).then_inc(done, 1)

            def tokens(step, r):
                if step == "affine_h":
                    ac.wait_ge(t["xhT"], r + 1)
                    nc.scalar.activation(act[:, 0, :], pb[:, 0:M], ACT.Identity, bias=lncol[:, 15:16],
                                         scale=lncol[:, 7:8]).then_inc(t["a1"], 1)
                if step == "copy_1":
                    copy2(t["xn2T"], t["a2"], r)
                if step == "exp":
                    ac.wait_ge(t["sub"], r + 1)
                    nc.scalar.activation(t1[:, :, :], t1[:, :, :], ACT.Exp, scale=SCALE).then_inc(t["ex"], 1)
                if step == "copy_heads":
                    copy2(t["ooT"], t["a3"], r)
                if step == "copy_2":
                    ac.wait_ge(t["xn3T"], r + 1)
                    nc.scalar.copy(xt_[:, bass.ds(r * M, M)], pb[:, 0:M])
                    nc.scalar.copy(act[:, 0, :], pb[:, 0:M])
                    nc.scalar.copy(xtb_[0:D1, bass.ds(r * M, M)], pb[0:D1, M:2 * M])
                    nc.scalar.copy(act[0:D1, 1, :], pb[0:D1, M:2 * M]).then_inc(t["a4"], 1)

            for n, (_, g) in enumerate(HEAD):
                square(n, n % 4, g, n < SQBUF)
                if n == LAG:
                    ac.wait_ge(s_lnc, 1)
                if n >= LAG:
                    gelu(n - LAG, (n - LAG) % 4, HEAD[n - LAG][1])
            ac.dma_start(b2c[:, :], a["L0_ffn_b2"][0:1, :]).then_inc(s_w1c, 16)
            ac.dma_start(W1c[:, :], w1_dram[0, 0:P, :]).then_inc(s_w1c, 16)
            ac.dma_start(W1cb[0:D1, :], w1_dram[0, P:D, :]).then_inc(s_w1c, 16)
            ac.dma_start(W1cb[D1:D1 + 1, :], b1_dram[0:1, :]).then_inc(s_w1c, 16)
            for b in range(len(XBLOCKS)):
                ac.wait_ge(s_stored[b], 64)
            for e in range(NE):
                ac.dma_start(W2s[:, e, :, :], a["L0_ffn_W2"][e].rearrange("(f p) d -> p f d", p=P)).then_inc(s_w2, 16)
            with ac.Fori(2, NT) as i:
                for k, (_, g) in enumerate(BODY):
                    n = NHD + (i - 2) * NB + k
                    square(n, (NHD + k) % 4, g, False)
                    gelu(n - LAG, (NHD + k - LAG) % 4, BODY[k - LAG][1])
                    for step in AT[k]:
                        tokens(step, i - 2)
            def common_hidden(half, f):
                ac.wait_ge(c_up, half * NF + f + 1)
                nc.scalar.activation(hc[:, f, half * HALF * M:(half + 1) * HALF * M],
                                     ps[:, (half * NF + f) % 4, 0:HALF * M], ACT.Gelu).then_inc(c_act, 1)

            for k, steps in enumerate(LAST_STEPS):
                if k < NE_SLOTS:
                    now, before = ENDING[LAG + k], ENDING[k]
                    if now is not None:
                        square(now, now % 4, ALL[now][1], False)
                    if before is not None:
                        gelu(before, before % 4, ALL[before][1])
                for step, run in steps:
                    tokens(step, run)
                if k in COMMON_AT[:NF]:
                    common_hidden(0, COMMON_AT.index(k))
            common_hidden(1, 0)
            common_hidden(1, 1)

            ac.wait_ge(s_hot, 1)
            nc.scalar.activation(lgb[:, :, :], lgb[:, :, :], ACT.Exp).then_inc(s_exl, 1)
            for f in range(2, NF):
                common_hidden(1, f)

            def hidden(j, b, first=False):
                ac.wait_ge(e_up, j + 1)
                if not first:
                    ac.wait_ge(e_down, j - 1)
                nc.scalar.activation(ht[:, b, :], ps[:, 2 * b:2 * b + 2, :].rearrange("p k c -> p (k c)")[:, 0:DFF],
                                     ACT.Gelu).then_inc(e_act, 1)

            def store(j, b):
                ac.wait_ge(e_res, j + 1)
                ac.dma_start(ys_dram[bass.ds(j * P, P), :], ysb[:, b, :]).then_inc(s_ys[b], 16)

            hidden(0, 0, True)
            hidden(1, 1, True)
            store(0, 0)
            with ac.Fori(1, (NTILE - 1) // 2) as k:
                hidden(2 * k, 0)
                store(2 * k - 1, 1)
                hidden(2 * k + 1, 1)
                store(2 * k, 0)
            hidden(NTILE - 1, 0)
            store(NTILE - 2, 1)
            store(NTILE - 1, 0)


_OUTS = [((64, 12, 192), "float32")]


def kernel(**inputs):
    import numpy as _np
    import concourse.bacc as _bacc
    from concourse import mybir as _mybir
    from concourse.bass_utils import run_bass_kernel_spmd as _run

    nc = _bacc.Bacc("TRN2", target_bir_lowering=False, num_devices=1)
    arrays, args = {}, {}
    for name in inputs:
        a = _np.ascontiguousarray(inputs[name])
        arrays[f"in_{name}_dram"] = a
        args[name] = nc.dram_tensor(f"in_{name}_dram", a.shape, _mybir.dt.from_np(a.dtype), kind="ExternalInput").ap()
    outs = []
    for i, (shape, dtype) in enumerate(_OUTS):
        outs.append(nc.dram_tensor(f"out_{i}_dram", shape, _mybir.dt.from_np(_np.dtype(dtype)), kind="ExternalOutput").ap())
    audio_tower(nc, args, outs[0])
    r = _run(nc, [arrays], core_ids=[0])
    return r.results[0]["out_0_dram"]
```

```python
import numpy as np
import concourse.bass as bass
from concourse import mybir
from contextlib import ExitStack

F32 = mybir.dt.float32
I32 = mybir.dt.int32
F32R = mybir.dt.float32r
ALU = mybir.AluOpType
ACT = mybir.ActivationFunctionType
X = mybir.AxisListType.X

P = 128
BATCH, SAMPLES = 64, 4000
C = 128
CONVS = [(10, 5), (3, 2), (3, 2), (3, 2), (3, 2), (2, 2), (2, 2)]
NT = 8
BT = BATCH // NT
D = 192
D1 = D - P
TOK = 12
M = BT * TOK
NH, HD = 6, 32
DFF, NE = 768, 9
NF = DFF // P
EPS = 1e-5
SCALE = float(HD) ** -0.5
TOKENS = BATCH * TOK
NTILE = (NE - 1) + (TOKENS - (NE - 1)) // P
ROWS = NTILE * P + TOKENS
WR = 2

PITCH = [800, 400, 200, 100, 50, 25, 12]
FLAT = [BT * p for p in PITCH]
LAST5 = 24

def cut(layer, per, counts, start=0):
    out = []
    for c in counts:
        out.append((layer, start, per, c))
        start += per * c
    return out

G0 = cut(0, 128, [3] * 14 + [4] * 2)
G1 = cut(1, 128, [4] * 4 + [3] * 3)
G2 = cut(2, 128, [4] * 2) + cut(2, 96, [3] * 2, 1024)
G3 = cut(3, 128, [4]) + cut(3, 96, [3], 512)
G4 = cut(4, 100, [4])
G5 = cut(5, 100, [2])
G6 = cut(6, M, [1])
GROUPS = [G0, G1, G2, G3, G4, G5, G6]
DELAY = [0, 1, 1, 2, 2, 2, 2]
ORDER = [1, 0, 1, 0, 1, 0, 3, 0, 1, 0, 3, 0, 0, 1, 0, 0, 4, 2, 0, 2, 0, 5, 1, 0, 0, 1, 0, 6, 2, 0, 2, 0]
LAG = 3
YBUF, SQBUF, XHBUF, TRBUF, XR = 4, 2, 2, 2, 4


def reads(group):
    layer, start, per, count = group
    if layer == 0:
        return 0, 0
    k, s = CONVS[layer]
    if layer == 6:
        return 0, FLAT[5]
    return s * start, min(s * (start + per * count - 1) + k, FLAT[layer - 1])


def feeds(a, b):
    lo, hi = reads(b)
    return a[0] == b[0] - 1 and a[1] < hi and a[1] + a[2] * a[3] > lo


BODY = [(DELAY[l], GROUPS[l][ORDER[:k].count(l)]) for k, l in enumerate(ORDER)]
assert all(ORDER.count(l) == len(GROUPS[l]) for l in range(7))
NB = len(BODY)
assert NB % 4 == 0, NB
HEAD = [(0, g) for g in G0] + [(1 - d, g) for d, g in BODY if d <= 1]
NHD = len(HEAD)
LOOP = [(i - d, g) for i in range(2, NT) for d, g in BODY]
TAIL_ORDER = [(1, 3), (1, 3), (0, 1), (0, 1), (0, 1), (1, 4), (0, 1), (0, 1), (0, 1), (1, 5), (0, 1), (0, 2), (0, 2),
              (1, 6), (0, 2), (0, 2), (0, 3), (0, 3), (0, 4), (0, 5), (0, 6)]
TAIL = [(NT - 1 - b, GROUPS[l][TAIL_ORDER[:k].count((b, l))]) for k, (b, l) in enumerate(TAIL_ORDER)]
assert sorted(TAIL) == sorted([(NT - d, g) for d, g in BODY if d >= 1] + [(NT + 1 - d, g) for d, g in BODY if d == 2])
ALL = HEAD + LOOP + TAIL
NG = len(ALL)
assert [s[1] for s in HEAD[-LAG:]] == [s[1] for s in BODY[-LAG:]]


def last_feed(n):
    return max((m for m in range(n) if ALL[m][0] == ALL[n][0] and feeds(ALL[m][1], ALL[n][1])), default=None)


BACK = [None if g[0] == 0 else min(n - last_feed(n) for n in range(NHD + k, NG - len(TAIL), NB))
        for k, (_, g) in enumerate(BODY)]
assert all(b is None or b > LAG for b in BACK)
for w, (tile, g) in enumerate(ALL):
    assert all(r <= w + LAG for r, s in enumerate(ALL) if s[0] == tile - 1 and feeds(g, s[1])), (w, g)
H6_BACK = NB - ORDER.index(6)


SLOT = {"turn_h": 0, "stat_h": 0, "power_h": 0, "norm_h": 2, "turn_norm_h": 5, "affine_h": 5, "project": 6,
        "stat_1": 6, "power_1": 6, "norm_1": 7, "turn_1": 9, "copy_1": 9, "qkv": 11, "split_heads": 11,
        "scores": 13, "mask": 13, "less_max": 14, "exp": 16, "turn_probs": 17, "copy_probs": 17, "values": 19,
        "divide": 19, "turn_heads": 22, "copy_heads": 24, "out_project": 25, "residual": 25, "power_2": 25,
        "norm_2": 26, "turn_2": 28, "copy_2": 29, "logits": 31, "keep_logits": 31}
STEPS = list(SLOT)
AT = [[step for step in STEPS if SLOT[step] == k] for k in range(NB)]
RUNS = NT + 1
PER_SLOT = 2


def spread():
    slots = list(range(NG - len(TAIL) - LAG, NG - len(TAIL)))
    for n in range(NG - len(TAIL), NG):
        while slots[-LAG:].count(last_feed(n)):
            slots.append(None)
        slots.append(n)
    return slots + [None] * LAG


ENDING = spread()
NE_SLOTS = len(ENDING) - LAG
LAST_STEPS = [[] for _ in range(NE_SLOTS)]
starts = []
free = 0
for run, n6 in ((NT - 2, None), (NT - 1, ALL.index((NT - 2, G6[0]))), (NT, NG - 1)):
    if n6 is not None:
        free = max(free, ENDING.index(n6) + 1)
    starts.append(free)
    for k, step in enumerate(STEPS):
        while len(LAST_STEPS) <= free:
            LAST_STEPS.append([])
        LAST_STEPS[free].append((step, run))
        if (k + 1) % PER_SLOT == 0:
            free += 1
PARTS = ((0, 3), (3, 6), (6, NT))
ITEMS = [(p, f, None) if f is not None else (p, None, i)
         for p, (lo, hi) in enumerate(PARTS) for f, i in [(f, None) for f in range(NF)] + [(None, i) for i in range(lo, hi)]]
UPS = [sum(1 for x in ITEMS[:k] if x[1] is not None) for k in range(len(ITEMS) + 1)]
ITEM_AT, at = [], ENDING.index(ALL.index((NT - 1, G3[0]))) - LAG
for p, f, i in ITEMS:
    if p == len(PARTS) - 1:
        break
    at = max(at, starts[p + 1]) + 1
    ITEM_AT.append(at)
while len(LAST_STEPS) < ITEM_AT[-1] + 2:
    LAST_STEPS.append([])
CBANK = (2, 3)
N_LAST = ALL.index((NT - 1, G3[0]))


def bank(n):
    return n % 4 if n < N_LAST else n % 2


XPP = BT * SAMPLES // P
XBLOCKS = ((0, 1), (1, 2), (2, NT))
K0 = CONVS[0][0]
XCOLS = [max(5 * g[2] * g[3] for g in G0[r::XR]) for r in range(XR)]
W_TAPS = [(l, t) for l in range(1, 7) for t in range(CONVS[l][0])]
TAP0 = {l: W_TAPS.index((l, 0)) for l in range(1, 7)}
NTAP = len(W_TAPS)
TAPS_AT = (8, 10, 12, 13)
assert NTAP == 4 * len(TAPS_AT)


def audio_tower(nc, a, out):
    ctx = ExitStack()
    with ctx:
        def sb(name, shape, dt=F32):
            return ctx.enter_context(nc.sbuf_tensor(name, shape, dt))

        def sem(name):
            return ctx.enter_context(nc.semaphore(name))

        h = [sb(f"h{l}", [P, FLAT[l] + (l < 4) if l < 5 else BT * LAST5]) for l in range(6)]
        h6 = sb("h6", [P, M])
        xring = sb("xring", [4 * K0, sum(XCOLS)], F32R)
        xr = [xring[:, sum(XCOLS[:r]):sum(XCOLS[:r + 1])] for r in range(XR)]
        w0t = sb("w0t", [4 * K0, C], F32R)
        w0c = sb("w0c", [4 * K0, C])
        w0h = sb("w0h", [4 * K0, C], F32R)
        w0m = sb("w0m", [4 * K0, 2])
        wt = sb("wt", [P, NTAP, C])
        wraw = h[1][:, 0:NTAP * C].rearrange("p (t c) -> p t c", c=C)
        w0raw = sb("w0raw", [P, 4, K0])
        lnraw = sb("lnraw", [16, C])
        lncol = sb("lncol", [P, 16])
        wmean = sb("wmean", [P, 4])
        wscaled = sb("wscaled", [P, 4])
        ident = sb("ident", [P, P])
        mask = sb("mask", [M, M])
        spare = sb("r0", [1, 3])
        hsum_a, hsum_b, hsum = (sb(name, [M, NT, NE]) for name in ("hsum_a", "hsum_b", "hsum"))
        neghalf = sb("neghalf", [P, 4])
        eps = sb("eps", [P, 1])
        ceps = sb("ceps", [P, 4])
        sq = sb("sq", [P, SQBUF, 512])
        xh = sb("xh", [P, XHBUF, 512])
        ssum = sb("ssum", [P, YBUF, 4])
        varv = sb("varv", [P, YBUF, 4])
        rstd = sb("rstd", [P, YBUF, 4])

        projw = sb("projw", [P, D])
        projb = sb("projb", [1, D])
        wqkv = sb("wqkv", [P, 2, 3 * D])
        wprj = sb("wprj", [P, 2, D])
        wsr = sb("wsr", [P, 2, NE])
        ones = sb("ones", [1, P])
        iota = sb("iota", [M, NE])
        W1c = sb("W1c", [P, DFF])
        W1cb = sb("W1cb", [D1 + 1, DFF])
        W1r = h[1][:, 0:WR * DFF].rearrange("p (r c) -> p r c", r=WR)
        W1rb = h[1][0:D1 + 1, WR * DFF:2 * WR * DFF].rearrange("p (r c) -> p r c", r=WR)
        W2s = sb("W2s", [P, NE, NF, D])
        b2c = sb("b2c", [1, D])
        b2s = wt[0:1, :, :].rearrange("p t c -> p (t c)")[:, 0:NE * D]
        flat2 = W2s[:, :, :, :].rearrange("p e f d -> p (e f d)")
        xraw, xhi, xlo = (flat2[:, j * NT * XPP:(j + 1) * NT * XPP] for j in range(3))
        xt_ = sb("xt", [P, RUNS * M])
        xtb_ = sb("xtb", [D1 + 1, RUNS * M])
        acc_ = sb("acc", [M, RUNS, D])
        xt, xtb, acc = xt_[:, M:RUNS * M], xtb_[:, M:RUNS * M], acc_[:, 1:RUNS, :]

        stats = sb("stats", [M, 6])
        mv = sb("mv", [M, 2])
        veps = sb("veps", [M, 1])
        rs = sb("rs", [M, 1])
        xn = sb("xn", [M, D])
        act = sb("act", [P, 2, M])
        x1 = sb("x1", [M, D])
        qm = sb("qm", [P, NH, M])
        kT = sb("kT", [P, 2, M])
        vv = sb("vv", [M, D])
        scores = sb("t1", [M, NH, M])
        mx = sb("mx", [M, NH])
        den = sb("den", [M, NH])
        rden = sb("rden", [M, NH])
        pT = sb("pT", [M, NH, M])
        oo = sb("oo", [M, D])
        hc = h[0][:, 0:NF * TOKENS].rearrange("p (f t) -> p f t", f=NF)
        ht = h[2][:, 0:2 * DFF].rearrange("p (b f) -> p b f", b=2)
        xs = h[3][:, 0:2 * D].rearrange("p (b d) -> p b d", b=2)
        xst = h[3][:, 2 * D:2 * D + 2 * P].rearrange("p (b t) -> p b t", b=2)
        xstb = sb("xstb", [D1 + 1, 2, P])
        ysb = h[4][:, 0:2 * D].rearrange("p (b d) -> p b d", b=2)
        kept = h[0][0:M, NF * TOKENS:NF * TOKENS + NT * D].rearrange("p (i d) -> p i d", i=NT)
        sel = h[0][0:M, NF * TOKENS:NF * TOKENS + NT * D].rearrange("p (i d) -> p i d", i=NT)
        xn3_ = sb("xn3", [M, RUNS, D + 1])
        xn3 = xn3_[:, 1:RUNS, :]
        zero = sb("zero", [P, D + 1])
        numbers = sb("numbers", [P, NTILE])
        lga_ = sb("lga", [M, RUNS, NE])
        lga = lga_[:, 1:RUNS, :]
        lgb = sb("lgb", [M, NT, NE])
        hot = sb("hot", [M, NT, NE])
        route = sb("r8", [M, 8, NT])
        c0 = sb("c0", [M, NT])
        upper = sb("upper", [M, M])
        onesm = sb("onesm", [M, M])
        full = sb("full", [M, NE, TOKENS // P])
        below = sb("below", [M, NE, NE])
        dump = sb("dump", [M, NE])
        jota = sb("jota", [1, NTILE, NE])
        tiles3 = sb("tiles3", [M, NE, TOKENS // P])
        tiles = sb("tiles", [M, NE])
        base3 = sb("base3", [M, NE, NE])
        basev = sb("basev", [M, NE])
        base2 = sb("base2", [M, NE])
        upto = sb("upto", [1, NE])
        own3 = sb("own3", [1, NTILE, NE])
        ownf = sb("ownf", [1, NTILE])
        owni = sb("owni", [1, NTILE], mybir.dt.int32)
        slotf = sb("slotf", [M, NT])
        sloti = sb("sloti", [M, NT], mybir.dt.uint32)
        xparts = nc.dram_tensor("sample_parts", [4, BATCH * SAMPLES], F32, kind="Internal").ap()
        sorted_dram = nc.dram_tensor("sorted_tokens", [ROWS, D + 1], F32, kind="Internal").ap()
        results_dram = nc.dram_tensor("chosen_results", [TOKENS + P, D], F32, kind="Internal").ap()

        ps = ctx.enter_context(nc.psum_tensor("ps", [P, 8, 512], F32))
        y = [ps[:, i, :] for i in range(4)]
        tr = [ps[:, 4 + i, :] for i in range(2)]
        pa, pb = ps[:, 6, :], ps[:, 7, :]

        taps_here = sem("taps_here")
        scales_here = sem("scales_here")
        offsets_here = sem("offsets_here")
        identity_made = sem("identity_made")
        constants_made = sem("constants_made")
        w0_here = sem("w0_here")
        samples_here = [sem(f"samples_here{b}") for b in range(len(XBLOCKS))]
        parts_stored = [sem(f"parts_stored{b}") for b in range(len(XBLOCKS))]
        high_parts = sem("high_parts")
        both_parts = sem("both_parts")
        w0_masks_made = sem("w0_masks")
        w0_steps = sem("w0_steps")
        w0_ready = sem("w0_ready")
        tokens_done = sem("tokens_done")
        tokens_kept = sem("tokens_turned_kept")
        pads_made = sem("pads_made")
        weights_turned = sem("weights_turned")
        weights_summed = sem("weights_summed")
        weight_means = sem("weight_means")
        weights_centred = sem("weights_centred")
        columns_ready = sem("columns_ready")
        samples_in_ring = [sem(f"samples_in_ring{i}") for i in range(XR)]
        conv_done = sem("conv_done")
        sq_done = sem("sq_done")
        ssum_done = sem("ssum_done")
        varv_done = sem("varv_done")
        rstd_done = sem("rstd_done")
        xh_done = sem("xh_done")
        tr_done = sem("tr_done")
        act_done = sem("act_done")
        token_weights_here = sem("token_weights_here")
        t = {"h6r": sem("h_turned"), "st1": sem("h_stats"), "mv1": sem("h_mean_var"), "ve1": sem("h_var_eps"),
             "rs1": sem("h_power"), "xh1": sem("h_normed"), "xhT": sem("normed_h_turned"),
             "a1": sem("normed_h_scaled"), "pj": sem("projected"), "x1": sem("projected_kept"),
             "st2": sem("stats_1"), "mv2": sem("mean_var_1"), "ve2": sem("var_eps_1"), "rs2": sem("power_1"),
             "xn2": sem("normed_1"), "xn2T": sem("normed_1_turned"), "a2": sem("normed_1_copied"),
             "qkv": sem("qkv_done"), "qk": sem("heads_split"), "sc": sem("scores_done"),
             "msk": sem("scores_masked"), "mx": sem("maxima"), "sub": sem("less_maxima"),
             "ex": sem("exponentials"), "den": sem("denominators"), "rden": sem("reciprocals"),
             "pT": sem("probs_turned"), "pTc": sem("probs_copied"), "pv": sem("values_done"),
             "oo": sem("heads_divided"), "ooT": sem("heads_turned"), "a3": sem("heads_copied"),
             "at": sem("out_projected"), "x2": sem("residual_done"), "st3": sem("stats_2"),
             "mv3": sem("mean_var_2"), "ve3": sem("var_eps_2"), "rs3": sem("power_2"), "xn3": sem("normed_2"),
             "xn3T": sem("normed_2_turned"), "a4": sem("normed_2_copied"), "lo": sem("logits_done")}
        second_weights_here = sem("second_weights_here")
        second_biases_here = sem("second_biases_here")
        zeros_made = sem("zeros_made")
        rows_cleared = sem("rows_cleared")
        routing_constants = sem("routing_constants")
        c_up = sem("common_up_done")
        c_act = sem("common_hidden_done")
        c_out = sem("common_down_done")
        c_kept = sem("common_kept")
        c_acc = sem("common_added")
        routing_steps = sem("routing_steps")
        exponentials_known = sem("routing_exponentials")
        chosen_known = sem("chosen_known")
        ranks_known = sem("ranks_known")
        sums_doubled = sem("sums_doubled")
        slots_known = sem("slots_known")
        owners_known = sem("owners_known")
        tokens_sorted = sem("tokens_sorted")
        first_weights_here = [sem(f"first_weights_here{k}") for k in range(WR)]
        tile_tokens_here = [sem(f"tile_tokens_here{k}") for k in range(2)]
        e_turn = sem("tile_turned")
        e_copy = sem("tile_copied")
        e_up = sem("tile_up_done")
        e_act = sem("tile_hidden_done")
        e_down = sem("tile_down_done")
        e_res = sem("tile_result_here")
        tile_stored = [sem(f"tile_stored{k}") for k in range(2)]
        numbers_here = sem("numbers_here")
        results_here = [sem(f"results_here{i}") for i in range(0, NT, 2)]
        sums_done = sem("sum_done")
        output_stored = sem("output_stored")

        block = ctx.enter_context(nc.Block())

        WEIGHTS = [(projw[:, :], a["L0_tok_proj_w"]), (projb[:, :], a["L0_tok_proj_b"].rearrange("(a c) -> a c", a=1))]
        for src, dst in ((a["L0_attn_w_qkv"], wqkv), (a["L0_attn_w_proj"], wprj), (a["L0_ffn_Ws"], wsr)):
            WEIGHTS += [(dst[:, 0, :], src[0:P, :]), (dst[0:D1, 1, :], src[P:D, :])]
        WEIGHTS.append((wsr[D1:D1 + 1, 1, :], a["L0_ffn_bs"].rearrange("(a c) -> a c", a=1)))
        WEIGHTS += [(b2c[:, :], a["L0_ffn_b2"][0:1, :]), (W1c[:, :], a["L0_ffn_W1"][0, 0:P, :]),
                    (W1cb[0:D1, :], a["L0_ffn_W1"][0, P:D, :]), (W1cb[D1:D1 + 1, :], a["L0_ffn_b1"][0:1, :])]

        def shifted(off, cols):
            return bass.AP(xparts.tensor, off, [[BATCH * SAMPLES, 4], [1, K0], [1, cols]])

        def tiles_of(rows, b):
            lo, hi = XBLOCKS[b]
            return rows[lo * BT * SAMPLES:hi * BT * SAMPLES].rearrange("(p c) -> p c", p=P)

        w1_dram, b1_dram = a["L0_ffn_W1"], a["L0_ffn_b1"]

        @block.sync
        def _(sp):
            xin = a["x"].rearrange("b s -> (b s)")
            for b, (lo, hi) in enumerate(XBLOCKS[:2]):
                sp.dma_start(xraw[:, lo * XPP:hi * XPP], tiles_of(xin, b)).then_inc(samples_here[b], 16)
                if b == 0:
                    sp.dma_start(w0raw[:, :, :], a["L0_tok_conv_w0"].rearrange("o i k -> o (i k)").unsqueeze(1)
                                 .to_broadcast([P, 4, K0])).then_inc(w0_here, 16)

            def load_x(i, g, read_by, short=False):
                _, start, per, count = G0[g]
                cols = 5 * per * count - (9 if short else 0)
                if read_by is not None:
                    sp.wait_ge(conv_done, read_by + 1)
                sp.dma_start(xr[g % XR][:, 0:cols].bitcast(F32), shifted(i * (BT * SAMPLES) + 5 * start, cols))\
                    .then_inc(samples_in_ring[g % XR], 16)

            def store_parts(b):
                lo, hi = XBLOCKS[b]
                sp.wait_ge(both_parts, b + 1)
                for j in range(4):
                    sp.dma_start(tiles_of(xparts[j], b), (xhi, xlo)[j % 2][:, lo * XPP:hi * XPP]).then_inc(parts_stored[b], 16)

            body_at = [ORDER.index(0)]
            while len(body_at) < len(G0):
                body_at.append(ORDER.index(0, body_at[-1] + 1))
            head_at = [n for n, s in enumerate(HEAD) if s[1][0] == 0]
            store_parts(0)
            for l in range(4, 8):
                name = f"L0_tok_ln_b{l}" if l < 7 else "L0_tok_fln_b"
                sp.dma_start(lnraw[8 + l:9 + l, :], a[name].rearrange("(a c) -> a c", a=1)).then_inc(scales_here, 16)
            sp.wait_ge(parts_stored[0], 64)
            for n in range(2 * len(G0)):
                i, g = n // len(G0), n % len(G0)
                if g == len(G0) - 1:
                    sp.wait_ge(parts_stored[i + 1], 64)
                load_x(i, g, head_at[n - XR] if n >= XR else None)
                if XR <= n < XR + 6:
                    l = n - XR + 1
                    k = CONVS[l][0]
                    sp.dma_start(wraw[:, TAP0[l]:TAP0[l] + k, :].rearrange("p t c -> p (t c)"),
                                 a[f"L0_tok_conv_w{l}"].rearrange("o i k -> o (i k)")).then_inc(taps_here, 16)
                if n == XR + 6:
                    store_parts(1)
                if n == XR + 7:
                    lo, hi = XBLOCKS[2]
                    sp.dma_start(xraw[:, lo * XPP:hi * XPP], tiles_of(xin, 2)).then_inc(samples_here[2], 16)
                if n == len(G0) + XR:
                    store_parts(2)
                e = n - (2 * len(G0) - NE)
                if e == 0:
                    for b in range(len(XBLOCKS)):
                        sp.wait_ge(parts_stored[b], 64)
                if e >= 0:
                    sp.dma_start(W2s[:, e, :, :], a["L0_ffn_W2"][e].rearrange("(f p) d -> p f d", p=P)).then_inc(second_weights_here, 16)
                if XR + 8 <= n < XR + 8 + len(WEIGHTS):
                    dst, src = WEIGHTS[n - XR - 8]
                    sp.dma_start(dst, src).then_inc(token_weights_here, 16)
            for g in range(XR):
                load_x(2, g, head_at[2 * len(G0) + g - XR])

            def later(i, last):
                step = NHD + (i - 2) * NB
                for g in range(XR, len(G0)):
                    load_x(i, g, step + body_at[g - XR], short=last and g == len(G0) - 1)
                if not last:
                    for g in range(XR):
                        load_x(i + 1, g, step + body_at[len(G0) + g - XR])

            with sp.Fori(2, NT - 1) as i:
                later(i, False)
            later(NT - 1, True)

            sp.wait_ge(act_done, NG)
            sp.dma_start(b2s, a["L0_ffn_b2"].rearrange("e d -> (e d)").rearrange("(a c) -> a c", a=1)).then_inc(second_biases_here, 16)
            sp.wait_ge(owners_known, 1)

            def load_weights(j, b, first):
                own = sp.value_load(owni[0:1, bass.ds(j, 1)], min_val=0, max_val=NE - 1)
                if not first:
                    sp.wait_ge(e_up, j - WR + 1)
                sp.dma_start(W1r[:, b, :], w1_dram[bass.ds(own, 1), 0:P, :].rearrange("e p n -> p (e n)")).then_inc(first_weights_here[b], 16)
                sp.dma_start(W1rb[0:D1, b, :], w1_dram[bass.ds(own, 1), P:D, :].rearrange("e p n -> p (e n)")).then_inc(first_weights_here[b], 16)
                sp.dma_start(W1rb[D1:D1 + 1, b, :], b1_dram[bass.ds(own, 1), :]).then_inc(first_weights_here[b], 16)

            def load_tokens(j, b, first):
                if not first:
                    sp.wait_ge(e_turn, j - 1)
                sp.dma_start(xs[:, b, :], sorted_dram[bass.ds(j * P, P), 0:D]).then_inc(tile_tokens_here[b], 16)

            for j in range(2):
                load_weights(j, j, True)
            sp.wait_ge(tokens_sorted, 16 * NT)
            for j in range(2):
                load_tokens(j, j, True)
            sp.dma_start(numbers[:, :].unsqueeze(2), sorted_dram[0:NTILE * P, D:D + 1].rearrange("(j p) n -> p j n", p=P),
                         allow_slow_non_contiguous=True).then_inc(numbers_here, 16)
            with sp.Fori(0, (NTILE - 3) // 2) as k:
                for b in range(2):
                    load_tokens(2 * k + b + 2, b, False)
                    load_weights(2 * k + b + 2, b, False)
            load_tokens(NTILE - 1, (NTILE - 1) % 2, False)
            load_weights(NTILE - 1, (NTILE - 1) % 2, False)
            for b in range(2):
                sp.wait_ge(tile_stored[b], 16 * ((NTILE - b + 1) // 2))
            for i in range(0, NT, 2):
                sp.dma_start(sel[:, i:i + 2, :], results_dram[i * M:(i + 2) * M, :].rearrange("(i p) d -> p i d", p=M)).then_inc(results_here[i // 2], 16)
            for i in range(0, NT, 2):
                sp.wait_ge(sums_done, i + 2)
                sp.dma_start(out.rearrange("(i b) t d -> (b t) i d", i=NT)[:, i:i + 2, :], acc[:, i:i + 2, :]).then_inc(output_stored, 16)
            sp.wait_ge(output_stored, 16 * NT // 2)

        @block.gpsimd
        def _(gp):
            gp.memset(ident[:, :], 0.0).then_inc(identity_made, 1)
            gp.wait_ge(identity_made, 1)
            gp.affine_select(out=ident[:, :], in_=ident[:, :], compare_op=ALU.not_equal, fill=1.0,
                             base=0, pattern=[[-1, P]], channel_multiplier=1).then_inc(identity_made, 1)
            gp.memset(w0m[:, :], 1.0).then_inc(w0_masks_made, 1)
            gp.wait_ge(w0_masks_made, 1)
            gp.affine_select(out=w0m[:, 0:1], in_=w0m[:, 0:1], compare_op=ALU.is_ge, fill=0.0,
                             base=2 * K0 - 1, pattern=[[0, 1]], channel_multiplier=-1).then_inc(w0_masks_made, 1)
            gp.affine_select(out=w0m[:, 1:2], in_=w0m[:, 1:2], compare_op=ALU.is_ge, fill=0.0,
                             base=-2 * K0, pattern=[[0, 1]], channel_multiplier=1).then_inc(w0_masks_made, 2)
            gp.memset(neghalf[:, :], -0.5).then_inc(constants_made, 1)
            gp.memset(eps[:, :], EPS).then_inc(constants_made, 1)
            gp.memset(ceps[:, :], C * EPS).then_inc(constants_made, 1)
            for l in range(4):
                gp.dma_start(lnraw[8 + l:9 + l, :], a[f"L0_tok_ln_b{l}"].rearrange("(a c) -> a c", a=1)).then_inc(offsets_here, 16)
            gp.wait_ge(constants_made, 3)

            def group(n, idx, g):
                _, _, per, count = g
                gp.wait_ge(ssum_done, n + 1)
                gp.tensor_tensor(varv[0:per, idx, 0:count], ssum[0:per, idx, 0:count], ceps[0:per, 0:count],
                                 ALU.add).then_inc(varv_done, 1)
                gp.wait_ge(varv_done, n + 1)
                gp.tensor_tensor(rstd[0:per, idx, 0:count], varv[0:per, idx, 0:count],
                                 neghalf[0:per, 0:count], ALU.pow).then_inc(rstd_done, 1)

            def power(tag, r):
                gp.wait_ge(t["mv" + tag], r + 1)
                gp.tensor_tensor(veps[:, :], mv[:, 1:2], eps[0:M, :], ALU.add).then_inc(t["ve" + tag], 1)
                gp.wait_ge(t["ve" + tag], r + 1)
                gp.tensor_tensor(rs[:, :], veps[:, :], neghalf[0:M, 0:1], ALU.pow).then_inc(t["rs" + tag], 1)

            def tokens(step, r):
                for name, tag in (("power_h", "1"), ("power_1", "2"), ("power_2", "3")):
                    if step == name:
                        power(tag, r)

            for n, (_, g) in enumerate(HEAD):
                group(n, n % 4, g)
                if n == len(G0) + 6:
                    gp.memset(mask[:, :], 0.0).then_inc(constants_made, 1)
                    gp.wait_ge(constants_made, 4)
                    mv3 = mask[:, :].rearrange("p (j c) -> p j c", c=TOK)
                    gp.affine_select(out=mv3, in_=mv3, compare_op=ALU.is_ge, fill=-1e30,
                                     base=0, pattern=[[-TOK, BT], [0, TOK]], channel_multiplier=1).then_inc(constants_made, 1)
                    gp.wait_ge(constants_made, 5)
                    gp.affine_select(out=mv3, in_=mv3, compare_op=ALU.is_ge, fill=-1e30,
                                     base=TOK - 1, pattern=[[TOK, BT], [0, TOK]], channel_multiplier=-1).then_inc(constants_made, 1)
                    gp.iota(iota[:, :], pattern=[[1, NE]], base=0, channel_multiplier=0,
                            allow_small_or_imprecise_dtypes=True).then_inc(constants_made, 1)
                if n == len(G0) + 10:
                    gp.memset(zero[:, :], 0.0).then_inc(zeros_made, 1)
                    gp.wait_ge(zeros_made, 1)
                    gp.iota(zero[:, D:D + 1].bitcast(I32), pattern=[[0, 1]], base=TOKENS, channel_multiplier=1).then_inc(zeros_made, 1)
                    gp.iota(xn3[:, :, D].bitcast(I32), pattern=[[M, NT]], base=0, channel_multiplier=1).then_inc(zeros_made, 1)
                    gp.wait_ge(zeros_made, 3)
                    gp.dma_start(sorted_dram[0:NTILE * P, :].rearrange("(j p) d -> p j d", p=P),
                                 zero[:, :].unsqueeze(1).to_broadcast([P, NTILE, D + 1])).then_inc(rows_cleared, 16)
                if n == len(G0) + 14:
                    gp.dma_start(results_dram[0:TOKENS, :].rearrange("(j p) d -> p j d", p=P),
                                 zero[:, 0:D].unsqueeze(1).to_broadcast([P, TOKENS // P, D])).then_inc(rows_cleared, 16)
                if n == len(G0) + 18:
                    gp.memset(upper[:, :], 1.0).then_inc(routing_constants, 1)
                    gp.memset(onesm[:, :], 1.0).then_inc(routing_constants, 1)
                    gp.memset(below[:, :, :], 1.0).then_inc(routing_constants, 1)
                    gp.memset(dump[:, :], 0.0).then_inc(routing_constants, 1)
                    gp.wait_ge(routing_constants, 4)
                    gp.affine_select(out=upper[:, :], in_=upper[:, :], compare_op=ALU.is_gt, fill=0.0,
                                     base=0, pattern=[[1, M]], channel_multiplier=-1).then_inc(routing_constants, 1)
                    gp.affine_select(out=below[:, :, :], in_=below[:, :, :], compare_op=ALU.is_gt, fill=0.0,
                                     base=0, pattern=[[1, NE], [-1, NE]], channel_multiplier=0).then_inc(routing_constants, 1)
                    gp.wait_ge(routing_constants, 6)
                    gp.memset(below[:, :, 0:1], 0.0).then_inc(routing_constants, 1)
                    gp.memset(dump[:, 0:1], float(NTILE)).then_inc(routing_constants, 1)
                    gp.iota(full[:, :, :], pattern=[[0, NE], [P, TOKENS // P]], base=0, channel_multiplier=0,
                            allow_small_or_imprecise_dtypes=True).then_inc(routing_constants, 1)
                    gp.iota(jota[:, :, :], pattern=[[1, NTILE], [0, NE]], base=0, channel_multiplier=0,
                            allow_small_or_imprecise_dtypes=True).then_inc(routing_constants, 1)
            with gp.Fori(2, NT) as i:
                for k, (_, g) in enumerate(BODY):
                    group(NHD + (i - 2) * NB + k, (NHD + k) % 4, g)
                    for step in AT[k]:
                        tokens(step, i - 2)
            for k, steps in enumerate(LAST_STEPS):
                if k < NE_SLOTS and ENDING[LAG + k] is not None:
                    n = ENDING[LAG + k]
                    group(n, bank(n), ALL[n][1])
                for step, run in steps:
                    tokens(step, run)

            gp.wait_ge(rows_cleared, 32)
            gp.wait_ge(slots_known, 1)
            for i in range(NT):
                gp.indirect_dma_start(out=sorted_dram[:, :], out_offset=bass.IndirectOffsetOnAxis(ap=sloti[:, i:i + 1], axis=0),
                                      in_=xn3[:, i, :], in_offset=None).then_inc(tokens_sorted, 16)
            gp.wait_ge(numbers_here, 16)
            for j in range(NTILE):
                gp.wait_ge(e_res, j + 1)
                if j >= 1:
                    gp.wait_ge(tile_stored[(j - 1) % 2], 16 * ((j - 1) // 2 + 1))
                gp.indirect_dma_start(out=results_dram[:, :], out_offset=bass.IndirectOffsetOnAxis(ap=numbers[:, j:j + 1].bitcast(mybir.dt.uint32), axis=0),
                                      in_=ysb[:, j % 2, :], in_offset=None).then_inc(tile_stored[j % 2], 16)

        @block.tensor
        def _(pe):
            pe.wait_ge(identity_made, 2)
            pe.wait_ge(w0_here, 16)
            nc.tensor.transpose(ps[0:4 * K0, 4, 0:C], w0raw[:, :, :].rearrange("p j k -> p (j k)"), ident[:, :]).then_inc(weights_turned, 1)
            pe.wait_ge(w0_ready, 1)

            def turn_taps(q):
                if q == 0:
                    pe.wait_ge(taps_here, 16 * 6)
                if q >= 2:
                    pe.wait_ge(weights_centred, q)
                for j in range(4):
                    l, tap = W_TAPS[4 * q + j]
                    k = CONVS[l][0]
                    src = wraw[:, TAP0[l]:TAP0[l] + k, :].rearrange("p t c -> p (t c)")\
                        .rearrange("p (c t) -> p t c", t=k)[:, tap, :]
                    last = nc.tensor.transpose(ps[:, 6 + q % 2, j * C:(j + 1) * C], src, ident[:, :])
                last.then_inc(weights_turned, 1)

            def conv(n, idx, g, tile, feed, early):
                layer, start, per, count = g
                if not early:
                    pe.wait_ge(xh_done, n - YBUF + 1)
                if layer == 0:
                    gi = G0.index(g)
                    pe.wait_ge(samples_in_ring[gi % XR], xwait(tile, gi))
                    for j in range(count):
                        last = nc.tensor.matmul(y[idx][0:per, j * C:(j + 1) * C],
                                                xr[gi % XR][:, 5 * per * j:5 * per * (j + 1):5], w0t[:, :],
                                                start=True, stop=True)
                    last.then_inc(conv_done, 1)
                    return
                pe.wait_ge(act_done, feed + 1)
                taps, st = CONVS[layer]
                for j in range(count):
                    for tap in range(taps):
                        lo = st * (start + per * j) + tap
                        src = h[layer - 1][:, lo:lo + st * (per - 1) + 1:st]
                        last = nc.tensor.matmul(y[idx][0:per, j * C:(j + 1) * C], src, wt[:, TAP0[layer] + tap, :],
                                                start=(tap == 0), stop=(tap == taps - 1))
                last.then_inc(conv_done, 1)

            def xwait(i, gi):
                return (i * (len(G0) // XR) + gi // XR + 1) * 16

            def turn(n, idx, g, early):
                _, _, per, count = g
                pe.wait_ge(xh_done, n + 1)
                if not early:
                    pe.wait_ge(act_done, n - TRBUF + 1)
                for j in range(count):
                    last = nc.tensor.transpose(tr[idx % TRBUF][:, j * per:(j + 1) * per],
                                               xh[0:per, idx % XHBUF, j * C:(j + 1) * C], ident[0:per, 0:per])
                last.then_inc(tr_done, 1)

            def turn2(src, ready, done, r):
                pe.wait_ge(ready, r + 1)
                nc.tensor.transpose(pb[:, 0:M], src[:, 0:P], ident[0:M, 0:M])
                nc.tensor.transpose(pb[0:D1, M:2 * M], src[:, P:D], ident[0:M, 0:M]).then_inc(done, 1)

            def tokens(step, r, h6_ready):
                if step == "turn_h":
                    pe.wait_ge(act_done, h6_ready)
                    nc.tensor.transpose(pa[0:M, 0:C], h6[:, :], ident[:, :]).then_inc(t["h6r"], 1)
                if step == "turn_norm_h":
                    pe.wait_ge(t["xh1"], r + 1)
                    pe.wait_ge(tokens_kept, r + 1)
                    nc.tensor.transpose(pb[:, 0:M], xn[:, 0:C], ident[0:M, 0:M]).then_inc(t["xhT"], 1)
                if step == "project":
                    pe.wait_ge(t["a1"], r + 1)
                    nc.tensor.matmul(pa[0:M, 0:D], act[:, 0, :], projw[:, :], start=True, stop=False)
                    nc.tensor.matmul(pa[0:M, 0:D], ones[0:1, 0:M], projb[0:1, :], start=False, stop=True).then_inc(t["pj"], 1)
                if step == "turn_1":
                    turn2(xn, t["xn2"], t["xn2T"], r)
                if step == "qkv":
                    pe.wait_ge(t["a2"], r + 1)
                    for j in range(4):
                        lo = (j // 2) * D + (j % 2) * P
                        w = D1 if j % 2 else P
                        o = pa[0:w, j * M:(j + 1) * M]
                        nc.tensor.matmul(o, wqkv[:, 0, lo:lo + w], act[:, 0, :], start=True, stop=False)
                        nc.tensor.matmul(o, wqkv[0:D1, 1, lo:lo + w], act[0:D1, 1, :], start=False, stop=True)
                    nc.tensor.matmul(pb[0:M, 0:D], act[:, 0, :], wqkv[:, 0, 2 * D:3 * D], start=True, stop=False)
                    nc.tensor.matmul(pb[0:M, 0:D], act[0:D1, 1, :], wqkv[0:D1, 1, 2 * D:3 * D], start=False, stop=True)\
                        .then_inc(t["qkv"], 1)
                if step == "scores":
                    pe.wait_ge(t["qk"], r + 1)
                    for hd in range(NH):
                        rows = P if hd < 4 else D1
                        last = nc.tensor.matmul((pa, pb)[hd // 3][0:M, (hd % 3) * M:(hd % 3 + 1) * M], qm[0:rows, hd, :],
                                                kT[0:rows, hd // 4, :], start=True, stop=True)
                    last.then_inc(t["sc"], 1)
                if step == "turn_probs":
                    pe.wait_ge(t["ex"], r + 1)
                    for hd in range(NH):
                        last = nc.tensor.transpose((pa, pb)[hd // 3][0:M, (hd % 3) * M:(hd % 3 + 1) * M], scores[:, hd, :],
                                                   ident[0:M, 0:M])
                    last.then_inc(t["pT"], 1)
                if step == "values":
                    pe.wait_ge(t["pTc"], r + 1)
                    for hd in range(NH):
                        last = nc.tensor.matmul(pa[0:M, hd * HD:(hd + 1) * HD], pT[:, hd, :], vv[:, hd * HD:(hd + 1) * HD],
                                                start=True, stop=True)
                    last.then_inc(t["pv"], 1)
                if step == "turn_heads":
                    turn2(oo, t["oo"], t["ooT"], r)
                if step == "out_project":
                    pe.wait_ge(t["a3"], r + 1)
                    nc.tensor.matmul(pa[0:M, 0:D], act[:, 0, :], wprj[:, 0, :], start=True, stop=False)
                    nc.tensor.matmul(pa[0:M, 0:D], act[0:D1, 1, :], wprj[0:D1, 1, :], start=False, stop=True).then_inc(t["at"], 1)
                if step == "turn_2":
                    turn2(xn, t["xn3"], t["xn3T"], r)
                if step == "logits":
                    pe.wait_ge(t["a4"], r + 1)
                    nc.tensor.matmul(pa[0:M, 0:NE], act[:, 0, :], wsr[:, 0, :], start=True, stop=False)
                    nc.tensor.matmul(pa[0:M, 0:NE], act[0:D1 + 1, 1, :], wsr[0:D1 + 1, 1, :], start=False, stop=True)\
                        .then_inc(t["lo"], 1)

            def common(k):
                p, f, i = ITEMS[k]
                lo, hi = PARTS[p]
                if f is not None and f == 0:
                    pe.wait_ge(tokens_kept, hi + 2)
                if k == 0:
                    pe.wait_ge(xh_done, N_LAST)
                    pe.wait_ge(second_weights_here, 16 * NE)
                elif k >= 2:
                    if ITEMS[k - 2][1] is not None:
                        pe.wait_ge(c_act, UPS[k - 1])
                    else:
                        pe.wait_ge(c_kept, k - 1 - UPS[k - 1])
                if f is not None:
                    o = ps[:, CBANK[k % 2], 0:(hi - lo) * M]
                    cols = slice(lo * M, hi * M)
                    nc.tensor.matmul(o, W1c[:, f * P:(f + 1) * P], xt[:, cols], start=True, stop=False)
                    nc.tensor.matmul(o, W1cb[:, f * P:(f + 1) * P], xtb[:, cols], start=False, stop=True).then_inc(c_up, 1)
                else:
                    if i == lo:
                        pe.wait_ge(c_act, UPS[k])
                    o = ps[0:M, CBANK[k % 2], 0:D]
                    for f in range(NF):
                        nc.tensor.matmul(o, hc[:, f, i * M:(i + 1) * M], W2s[:, 0, f, :], start=(f == 0), stop=False)
                    nc.tensor.matmul(o, ones[0:1, 0:M], b2c[0:1, :], start=False, stop=True).then_inc(c_out, 1)

            for n, (tile, g) in enumerate(HEAD):
                conv(n, n % 4, g, tile, last_feed(n), n < YBUF)
                if n == LAG - 1:
                    pe.wait_ge(scales_here, 16 * 12)
                    pe.wait_ge(offsets_here, 16 * 4)
                    nc.tensor.transpose(ps[:, 5, 0:16], lnraw[:, :], ident[0:16, 0:16]).then_inc(weights_turned, 1)
                if n == LAG:
                    pe.wait_ge(columns_ready, 1)
                if n >= LAG:
                    turn(n - LAG, (n - LAG) % 4, HEAD[n - LAG][1], n - LAG < TRBUF)
                if n in TAPS_AT:
                    turn_taps(TAPS_AT.index(n))
                if n == len(G0) - 1:
                    pe.wait_ge(weights_centred, 1 + NTAP // 4)
                    pe.wait_ge(pads_made, 4)
            pe.wait_ge(token_weights_here, 16 * len(WEIGHTS))
            pe.wait_ge(pads_made, 10)
            with pe.Fori(2, NT) as i:
                for k, (d, g) in enumerate(BODY):
                    n = NHD + (i - 2) * NB + k
                    conv(n, (NHD + k) % 4, g, i - d, None if BACK[k] is None else n - BACK[k], False)
                    turn(n - LAG, (NHD + k - LAG) % 4, BODY[k - LAG][1], False)
                    if k == 0:
                        pe.wait_ge(tokens_done, i - 1)
                    for step in AT[k]:
                        tokens(step, i - 2, n - H6_BACK + 1 if k == 0 else None)
            for k, steps in enumerate(LAST_STEPS):
                if k < NE_SLOTS:
                    now, before = ENDING[LAG + k], ENDING[k]
                    if now is not None:
                        if now >= N_LAST:
                            pe.wait_ge(xh_done, now - 1)
                        conv(now, bank(now), ALL[now][1], NT, last_feed(now), False)
                    if before is not None:
                        turn(before, bank(before), ALL[before][1], False)
                for step, run in steps:
                    if step == STEPS[0]:
                        pe.wait_ge(tokens_done, run + 1)
                    tokens(step, run, ALL.index((run - 1, G6[0])) + 1)
                if k in ITEM_AT:
                    common(ITEM_AT.index(k))
            pe.wait_ge(tokens_done, NT + 2)
            pe.wait_ge(tokens_kept, NT + 2)

            common(len(ITEM_AT))
            pe.wait_ge(routing_constants, 10)
            pe.wait_ge(chosen_known, 1)
            rank = pa[0:M, 0:NT * NE]
            nc.tensor.matmul(rank, upper[:, :], hot[:, :, :].rearrange("p i e -> p (i e)"), start=True, stop=False)
            pe.wait_ge(sums_doubled, 3)
            nc.tensor.matmul(rank[:, NE:NT * NE], onesm[:, :], hsum[:, 0:NT - 1, :].rearrange("p i e -> p (i e)"),
                             start=False, stop=True)
            nc.tensor.matmul(pb[0:M, 0:NE], onesm[:, :], hsum[:, NT - 1, :], start=True, stop=True).then_inc(ranks_known, 1)
            for k in range(len(ITEM_AT) + 1, len(ITEMS)):
                common(k)

            def turn_tile(j, half, b):
                pe.wait_ge(tile_tokens_here[b], 16 * (half + 1))
                if isinstance(j, int) and j == 0:
                    pe.wait_ge(chosen_known, 1)
                else:
                    pe.wait_ge(e_copy, j)
                nc.tensor.transpose(pb[:, 0:P], xs[:, b, 0:P], ident[:, :])
                nc.tensor.transpose(pb[0:D1, P:2 * P], xs[:, b, P:D], ident[:, :]).then_inc(e_turn, 1)

            def up(j, half, b, first=False):
                pe.wait_ge(e_copy, j + 1)
                pe.wait_ge(first_weights_here[b], 48 * (half + 1))
                if not first:
                    pe.wait_ge(e_act, j - 1)
                for f in range(NF):
                    o = ps[:, 2 * b + f // 4, (f % 4) * P:(f % 4 + 1) * P]
                    nc.tensor.matmul(o, W1r[:, b, f * P:(f + 1) * P], xst[:, b, :], start=True, stop=False)
                    last = nc.tensor.matmul(o, W1rb[:, b, f * P:(f + 1) * P], xstb[:, b, :], start=False, stop=True)
                last.then_inc(e_up, 1)

            def down(j, b, first=False):
                own = pe.value_load(owni[0:1, bass.ds(j, 1)], min_val=0, max_val=NE - 1)
                pe.wait_ge(e_act, j + 1)
                if not first:
                    pe.wait_ge(e_res, j - 1)
                o = ps[:, 4 + b, 0:D]
                for f in range(NF):
                    nc.tensor.matmul(o, ht[:, b, f * P:(f + 1) * P],
                                     W2s[:, bass.ds(own, 1), f, :].rearrange("p e d -> p (e d)"), start=(f == 0), stop=False)
                nc.tensor.matmul(o, ones[0:1, :], b2s[0:1, bass.ds(own * D, D)], start=False, stop=True).then_inc(e_down, 1)

            pe.wait_ge(owners_known, 1)
            turn_tile(0, 0, 0)
            pe.wait_ge(second_biases_here, 16)
            pe.wait_ge(c_kept, NT)
            turn_tile(1, 0, 1)
            up(0, 0, 0, True)
            turn_tile(2, 1, 0)
            up(1, 0, 1, True)
            down(0, 0, True)
            turn_tile(3, 1, 1)
            up(2, 1, 0)
            down(1, 1, True)
            with pe.Fori(1, (NTILE - 1) // 2 - 1) as k:
                turn_tile(2 * k + 2, k + 1, 0)
                up(2 * k + 1, k, 1)
                down(2 * k, 0)
                turn_tile(2 * k + 3, k + 1, 1)
                up(2 * k + 2, k + 1, 0)
                down(2 * k + 1, 1)
            L = NTILE - 1
            turn_tile(L, L // 2, 0)
            up(L - 1, (L - 1) // 2, 1)
            down(L - 2, 0)
            up(L, L // 2, 0)
            down(L - 1, 1)
            down(L, 0)

        @block.vector
        def _(ve):
            def part(b):
                lo, hi = (t * XPP for t in XBLOCKS[b])
                ve.wait_ge(samples_here[b], 16)
                nc.vector.tensor_copy(xhi[:, lo:hi].bitcast(F32R), xraw[:, lo:hi]).then_inc(high_parts, 1)
                ve.wait_ge(high_parts, b + 1)
                nc.vector.tensor_tensor(xlo[:, lo:hi].bitcast(F32R), xraw[:, lo:hi], xhi[:, lo:hi], ALU.subtract)\
                    .then_inc(both_parts, 1)

            def centre(done, dst, src, rows, cnt):
                if done:
                    ve.wait_ge(weights_centred, done)
                nc.vector.reduce_sum(wmean[0:rows, 0:cnt], src, axis=X).then_inc(weights_summed, 1)
                ve.wait_ge(weights_summed, done + 1)
                nc.vector.tensor_scalar(wscaled[0:rows, 0:cnt], wmean[0:rows, 0:cnt], 1.0 / C, None,
                                        ALU.mult).then_inc(weight_means, 1)
                ve.wait_ge(weight_means, done + 1)
                for j in range(cnt):
                    last = nc.vector.tensor_scalar(dst[:, j, :], src[:, j, :], wscaled[0:rows, j:j + 1], None, ALU.subtract)
                last.then_inc(weights_centred, 1)

            def centre_taps(q):
                ve.wait_ge(weights_turned, q + 3)
                centre(q + 1, wt[:, 4 * q:4 * q + 4, :], ps[:, 6 + q % 2, :].rearrange("p (t c) -> p t c", c=C), P, 4)

            part(0)
            ve.wait_ge(weights_turned, 1)
            centre(0, w0c[:, :].unsqueeze(1), ps[0:4 * K0, 4, 0:C].unsqueeze(1), 4 * K0, 1)
            ve.wait_ge(weights_centred, 1)
            nc.vector.tensor_copy(w0h[:, :], w0c[:, :]).then_inc(w0_steps, 1)
            ve.wait_ge(w0_steps, 1)
            nc.vector.tensor_tensor(w0c[:, :], w0c[:, :], w0h[:, :].bitcast(F32), ALU.subtract).then_inc(w0_steps, 1)
            ve.wait_ge(w0_steps, 2)
            ve.wait_ge(w0_masks_made, 4)
            nc.vector.tensor_scalar(w0c[:, :], w0c[:, :], w0m[:, 1:2], None, ALU.mult).then_inc(w0_steps, 1)
            ve.wait_ge(w0_steps, 3)
            nc.vector.scalar_tensor_tensor(out=w0t[:, :], in0=w0h[:, :].bitcast(F32), scalar=w0m[:, 0:1], in1=w0c[:, :],
                                           op0=ALU.mult, op1=ALU.add).then_inc(w0_ready, 1)
            part(1)
            for l in range(4):
                nc.vector.memset(h[l][:, FLAT[l]:FLAT[l] + 1], 0.0).then_inc(pads_made, 1)
            nc.vector.memset(ones[:, :], 1.0).then_inc(pads_made, 1)
            nc.vector.memset(h6[:, :], 0.0).then_inc(pads_made, 1)
            nc.vector.memset(xtb_[D1:D1 + 1, :], 1.0).then_inc(pads_made, 1)
            nc.vector.memset(act[D1:D1 + 1, 1, :], 1.0).then_inc(pads_made, 1)
            nc.vector.memset(xstb[D1:D1 + 1, :, :], 1.0).then_inc(pads_made, 1)
            nc.vector.memset(qm[:, :, :], 0.0).then_inc(pads_made, 1)

            def group(n, idx, g):
                _, _, per, count = g
                w = count * C
                ve.wait_ge(sq_done, n + 1)
                nc.vector.reduce_sum(ssum[0:per, idx, 0:count],
                                     sq[0:per, idx % SQBUF, 0:w].rearrange("p (j c) -> p j c", c=C), axis=X).then_inc(ssum_done, 1)

            def norm(n, idx, g, early):
                _, _, per, count = g
                w = count * C
                ve.wait_ge(rstd_done, n + 1)
                if not early:
                    ve.wait_ge(tr_done, n - XHBUF + 1)
                nc.vector.tensor_tensor(xh[0:per, idx % XHBUF, 0:w].rearrange("p (j c) -> p j c", c=C),
                                        y[idx][0:per, 0:w].rearrange("p (j c) -> p j c", c=C),
                                        rstd[0:per, idx, 0:count].unsqueeze(2).to_broadcast([per, count, C]),
                                        ALU.mult).then_inc(xh_done, 1)

            def stat(src, tag, wait, r):
                if wait is not None:
                    ve.wait_ge(wait, r + 1)
                nc.vector.bn_stats(stats[:, :], src).then_inc(t["st" + tag], 1)
                ve.wait_ge(pads_made, 10)
                ve.wait_ge(t["st" + tag], r + 1)
                nc.vector.bn_aggr(mv[:, :], stats[:, :]).then_inc(t["mv" + tag], 1)

            def normed(dst, src, tag, done, r):
                ve.wait_ge(t["rs" + tag], r + 1)
                nc.vector.tensor_scalar(dst, src, mv[:, 0:1], rs[:, 0:1], ALU.subtract, ALU.mult).then_inc(done, 1)

            def tokens(step, r):
                if step == "stat_h":
                    stat(pa[0:M, 0:C], "1", t["h6r"], r)
                if step == "norm_h":
                    normed(xn[:, 0:C], pa[0:M, 0:C], "1", t["xh1"], r)
                if step == "stat_1":
                    ve.wait_ge(t["pj"], r + 1)
                    nc.vector.tensor_copy(x1[:, :], pa[0:M, 0:D]).then_inc(t["x1"], 1)
                    stat(x1[:, :], "2", t["x1"], r)
                if step == "norm_1":
                    normed(xn[:, :], x1[:, :], "2", t["xn2"], r)
                if step == "split_heads":
                    ve.wait_ge(t["qkv"], r + 1)
                    for hd in range(NH):
                        lo = (hd % 4) * HD
                        nc.vector.tensor_copy(qm[lo:lo + HD, hd, :], pa[lo:lo + HD, (hd // 4) * M:(hd // 4 + 1) * M])
                    nc.vector.tensor_copy(kT[:, 0, :], pa[:, 2 * M:3 * M])
                    nc.vector.tensor_copy(kT[0:D1, 1, :], pa[0:D1, 3 * M:4 * M])
                    nc.vector.tensor_copy(vv[:, :], pb[0:M, 0:D]).then_inc(t["qk"], 1)
                if step == "mask":
                    ve.wait_ge(t["sc"], r + 1)
                    for half in range(2):
                        last = nc.vector.tensor_tensor(scores[:, 3 * half:3 * half + 3, :],
                                                       (pa, pb)[half][0:M, 0:3 * M].rearrange("p (h k) -> p h k", h=3),
                                                       mask[:, :].unsqueeze(1).to_broadcast([M, 3, M]), ALU.add)
                    last.then_inc(t["msk"], 1)
                    ve.wait_ge(t["msk"], r + 1)
                    nc.vector.reduce_max(mx[:, :], scores[:, :, :], axis=X).then_inc(t["mx"], 1)
                if step == "less_max":
                    ve.wait_ge(t["mx"], r + 1)
                    nc.vector.tensor_tensor(scores[:, :, :], scores[:, :, :], mx[:, :].unsqueeze(2).to_broadcast([M, NH, M]),
                                            ALU.subtract).then_inc(t["sub"], 1)
                if step == "turn_probs":
                    ve.wait_ge(t["ex"], r + 1)
                    nc.vector.reduce_sum(den[:, :], scores[:, :, :], axis=X).then_inc(t["den"], 1)
                    ve.wait_ge(t["den"], r + 1)
                    nc.vector.reciprocal(rden[:, :], den[:, :]).then_inc(t["rden"], 1)
                if step == "copy_probs":
                    ve.wait_ge(t["pT"], r + 1)
                    for half in range(2):
                        last = nc.vector.tensor_copy(pT[:, 3 * half:3 * half + 3, :],
                                                     (pa, pb)[half][0:M, 0:3 * M].rearrange("p (h k) -> p h k", h=3))
                    last.then_inc(t["pTc"], 1)
                if step == "divide":
                    ve.wait_ge(t["rden"], r + 1)
                    ve.wait_ge(t["pv"], r + 1)
                    nc.vector.tensor_tensor(oo[:, :].rearrange("p (h d) -> p h d", h=NH),
                                            pa[0:M, 0:D].rearrange("p (h d) -> p h d", h=NH),
                                            rden[:, :].unsqueeze(2).to_broadcast([M, NH, HD]), ALU.mult).then_inc(t["oo"], 1)
                if step == "residual":
                    ve.wait_ge(t["at"], r + 1)
                    nc.vector.tensor_tensor(x1[:, :], pa[0:M, 0:D], x1[:, :], ALU.add).then_inc(t["x2"], 1)
                    ve.wait_ge(t["x2"], r + 1)
                    stat(x1[:, :], "3", None, r)
                    nc.vector.tensor_copy(acc_[:, bass.ds(r, 1), :], x1[:, :].unsqueeze(1))
                if step == "norm_2":
                    normed(xn[:, :], x1[:, :], "3", t["xn3"], r)
                    nc.vector.tensor_scalar(xn3_[:, bass.ds(r, 1), 0:D], x1[:, :].unsqueeze(1), mv[:, 0:1], rs[:, 0:1],
                                            ALU.subtract, ALU.mult)
                if step == "keep_logits":
                    ve.wait_ge(t["lo"], r + 1)
                    nc.vector.tensor_copy(lga_[:, bass.ds(r, 1), :], pa[0:M, 0:NE].unsqueeze(1)).then_inc(tokens_done, 1)

            nc.vector.memset(spare[:, 0:1], 0.0).then_inc(tokens_done, 1)
            nc.vector.memset(spare[:, 1:2], 0.0).then_inc(tokens_kept, 1)
            def common_result(k):
                i = ITEMS[k][2]
                if i is not None:
                    ve.wait_ge(c_out, i + 1)
                    nc.vector.tensor_copy(kept[:, i, :], ps[0:M, CBANK[k % 2], 0:D]).then_inc(c_kept, 1)

            for n, (_, g) in enumerate(HEAD):
                group(n, n % 4, g)
                if n >= 1:
                    norm(n - 1, (n - 1) % 4, HEAD[n - 1][1], n - 1 < XHBUF)
                if n == LAG - 1:
                    ve.wait_ge(weights_turned, 2)
                    nc.vector.tensor_copy(lncol[:, 7:16], ps[:, 5, 7:16])
                    nc.vector.tensor_scalar(lncol[:, 0:7], ps[:, 5, 0:7], float(C) ** 0.5, None, ALU.mult).then_inc(columns_ready, 1)
                if n in TAPS_AT:
                    centre_taps(TAPS_AT.index(n))
                if n == len(G0):
                    part(2)
            ve.wait_ge(constants_made, 7)
            with ve.Fori(2, NT) as i:
                for k, (_, g) in enumerate(BODY):
                    n = NHD + (i - 2) * NB + k
                    group(n, (NHD + k) % 4, g)
                    norm(n - 1, (NHD + k - 1) % 4, BODY[k - 1][1], False)
                    for step in AT[k]:
                        tokens(step, i - 2)
            for k, steps in enumerate(LAST_STEPS):
                if k < NE_SLOTS:
                    now, before = ENDING[LAG + k], ENDING[LAG - 1 + k]
                    if now is not None:
                        group(now, bank(now), ALL[now][1])
                    if before is not None:
                        norm(before, bank(before), ALL[before][1], False)
                for step, run in steps:
                    tokens(step, run)
                if k - 1 in ITEM_AT:
                    common_result(ITEM_AT.index(k - 1))

            step = [0]

            def chain(ins):
                step[0] += 1
                ins.then_inc(routing_steps, 1)
                ve.wait_ge(routing_steps, step[0])

            def over(x, n=NE):
                return x.unsqueeze(2).to_broadcast([M, NT, n])

            ve.wait_ge(tokens_done, NT + 2)
            ve.wait_ge(routing_constants, 10)
            chain(nc.vector.reduce_max(route[:, 0, :], lga[:, :, :], axis=X))
            chain(nc.vector.tensor_tensor(lgb[:, :, :], lga[:, :, :], over(route[:, 0, :]), ALU.subtract))
            chain(nc.vector.tensor_scalar(lga[:, :, :], lgb[:, :, :], 0.0, 100.0, ALU.is_lt, ALU.mult))
            ioe = iota[:, :].unsqueeze(1).to_broadcast([M, NT, NE])
            chain(nc.vector.tensor_tensor(lga[:, :, :], lga[:, :, :], ioe, ALU.add))
            chain(nc.vector.tensor_reduce(route[:, 1, :], lga[:, :, :], axis=X, op=ALU.min))
            nc.vector.tensor_tensor(hot[:, :, :], ioe, over(route[:, 1, :]), ALU.is_equal).then_inc(chosen_known, 1)
            ve.wait_ge(chosen_known, 1)
            src = hot
            for k, dst in enumerate((hsum_a, hsum_b, hsum)):
                w = 1 << k
                nc.vector.tensor_copy(dst[:, 0:w, :], src[:, 0:w, :])
                nc.vector.tensor_tensor(dst[:, w:NT, :], src[:, w:NT, :], src[:, 0:NT - w, :], ALU.add).then_inc(sums_doubled, 1)
                ve.wait_ge(sums_doubled, k + 1)
                src = dst
            def shares():
                ve.wait_ge(exponentials_known, 1)
                chain(nc.vector.reduce_sum(route[:, 2, :], lgb[:, :, :], axis=X))
                chain(nc.vector.reciprocal(route[:, 3, :], route[:, 2, :]))
                chain(nc.vector.tensor_scalar(route[:, 4, :], route[:, 3, :], -1.0, 1.0, ALU.mult, ALU.add))
                chain(nc.vector.tensor_tensor(route[:, 5, :], route[:, 3, :], route[:, 2, :], ALU.mult))
                chain(nc.vector.tensor_tensor(route[:, 6, :], route[:, 5, :], route[:, 4, :], ALU.subtract))
                chain(nc.vector.tensor_tensor(route[:, 7, :], route[:, 6, :], hot[:, :, 0], ALU.mult))
                chain(nc.vector.tensor_tensor(c0[:, :], route[:, 7, :], route[:, 4, :], ALU.add))

            ve.wait_ge(ranks_known, 1)
            chain(nc.vector.tensor_tensor(tiles3[:, :, :], pb[0:M, 0:NE].unsqueeze(2).to_broadcast([M, NE, TOKENS // P]),
                                          full[:, :, :], ALU.is_gt))
            chain(nc.vector.reduce_sum(tiles[:, :], tiles3[:, :, :], axis=X))
            chain(nc.vector.tensor_tensor(base3[:, :, :], below[:, :, :], tiles[:, :].unsqueeze(1).to_broadcast([M, NE, NE]), ALU.mult))
            chain(nc.vector.reduce_sum(basev[:, :], base3[:, :, :], axis=X))
            chain(nc.vector.tensor_tensor(upto[:, :], basev[0:1, :], tiles[0:1, :], ALU.add))
            chain(nc.vector.tensor_tensor(own3[:, :, 1:NE], upto[:, 1:NE].unsqueeze(1).to_broadcast([1, NTILE, NE - 1]),
                                          jota[:, :, 1:NE], ALU.is_le))
            chain(nc.vector.reduce_sum(ownf[:, :], own3[:, :, 1:NE], axis=X))
            chain(nc.vector.tensor_scalar(ownf[:, :], ownf[:, :], 1.0, float(NE - 1), ALU.add, ALU.min))
            nc.vector.tensor_copy(owni[:, :], ownf[:, :]).then_inc(owners_known, 1)
            chain(nc.vector.tensor_tensor(basev[:, :], basev[:, :], dump[:, :], ALU.add))
            chain(nc.vector.tensor_scalar(base2[:, :], basev[:, :], float(P), None, ALU.mult))
            chain(nc.vector.tensor_tensor(lga[:, :, :], pa[0:M, 0:NT * NE].rearrange("p (i e) -> p i e", i=NT),
                                          base2[:, :].unsqueeze(1).to_broadcast([M, NT, NE]), ALU.add))
            ve.wait_ge(chosen_known, 1)
            chain(nc.vector.tensor_tensor(lga[:, :, :], lga[:, :, :], hot[:, :, :], ALU.mult))
            chain(nc.vector.reduce_sum(slotf[:, :], lga[:, :, :], axis=X))
            nc.vector.tensor_copy(sloti[:, :], slotf[:, :]).then_inc(slots_known, 1)

            for k in range(len(ITEM_AT), len(ITEMS)):
                common_result(k)
            def take(j, b, first=False):
                ve.wait_ge(e_turn, j + 1)
                if not first:
                    ve.wait_ge(e_up, j - 1)
                nc.vector.tensor_copy(xst[:, b, :], pb[:, 0:P])
                nc.vector.tensor_copy(xstb[0:D1, b, :], pb[0:D1, P:2 * P]).then_inc(e_copy, 1)

            def result(j, half, b, first=False):
                ve.wait_ge(e_down, j + 1)
                if not first:
                    ve.wait_ge(tile_stored[b], 16 * half)
                nc.vector.tensor_copy(ysb[:, b, :], ps[:, 4 + b, 0:D]).then_inc(e_res, 1)

            take(0, 0, True)
            take(1, 1, True)
            take(2, 0)
            result(0, 0, 0, True)
            take(3, 1)
            result(1, 0, 1, True)
            shares()
            for i in range(NT):
                ve.wait_ge(c_kept, i + 1)
                nc.vector.scalar_tensor_tensor(out=acc[:, i, :], in0=kept[:, i, :], scalar=c0[:, i:i + 1],
                                               in1=acc[:, i, :], op0=ALU.mult, op1=ALU.add).then_inc(c_acc, 1)
            with ve.Fori(1, (NTILE - 1) // 2 - 1) as k:
                take(2 * k + 2, 0)
                result(2 * k, k, 0)
                take(2 * k + 3, 1)
                result(2 * k + 1, k, 1)
            L = NTILE - 1
            take(L, 0)
            result(L - 2, (L - 2) // 2, 0)
            result(L - 1, (L - 1) // 2, 1)
            result(L, L // 2, 0)
            ve.wait_ge(c_acc, NT)
            for i in range(NT):
                ve.wait_ge(results_here[i // 2], 16)
                nc.vector.scalar_tensor_tensor(out=acc[:, i, :], in0=sel[:, i, :], scalar=route[:, 3, i:i + 1],
                                               in1=acc[:, i, :], op0=ALU.mult, op1=ALU.add).then_inc(sums_done, 1)

        @block.scalar
        def _(ac):
            for l in range(8):
                layer = f"L0_tok_ln_%s{l}" if l < 7 else "L0_tok_fln_%s"
                ac.dma_start(lnraw[l:l + 1, :], a[layer % "g"].rearrange("(a c) -> a c", a=1)).then_inc(scales_here, 16)
            ac.wait_ge(constants_made, 3)
            nc.scalar.activation(spare[:, 2:3], eps[0:1, :], ACT.Gelu)

            def square(n, idx, g, early):
                _, _, per, count = g
                w = count * C
                ac.wait_ge(conv_done, n + 1)
                if not early:
                    ac.wait_ge(ssum_done, n - SQBUF + 1)
                nc.scalar.activation(sq[0:per, idx % SQBUF, 0:w], y[idx][0:per, 0:w], ACT.Square).then_inc(sq_done, 1)

            def gelu(n, idx, g):
                layer, start, per, count = g
                w = count * per
                ac.wait_ge(tr_done, n + 1)
                src = tr[idx % TRBUF][:, 0:w]
                if layer == 6:
                    dst = h6[:, :]
                elif layer == 5:
                    src = src.rearrange("p (b q) -> p b q", b=BT)[:, :, 0:LAST5]
                    dst = h[5][:, :].rearrange("p (b q) -> p b q", b=BT)
                else:
                    dst = h[layer][:, start:start + w]
                nc.scalar.activation(dst, src, ACT.Gelu, bias=lncol[:, 8 + layer:9 + layer],
                                     scale=lncol[:, layer:layer + 1]).then_inc(act_done, 1)

            def copy2(wait, done, r):
                ac.wait_ge(wait, r + 1)
                nc.scalar.copy(act[:, 0, :], pb[:, 0:M])
                nc.scalar.copy(act[0:D1, 1, :], pb[0:D1, M:2 * M]).then_inc(done, 1)

            def tokens(step, r):
                if step == "affine_h":
                    ac.wait_ge(t["xhT"], r + 1)
                    nc.scalar.activation(act[:, 0, :], pb[:, 0:M], ACT.Identity, bias=lncol[:, 15:16],
                                         scale=lncol[:, 7:8]).then_inc(t["a1"], 1)
                if step == "copy_1":
                    copy2(t["xn2T"], t["a2"], r)
                if step == "exp":
                    ac.wait_ge(t["sub"], r + 1)
                    nc.scalar.activation(scores[:, :, :], scores[:, :, :], ACT.Exp, scale=SCALE).then_inc(t["ex"], 1)
                if step == "copy_heads":
                    copy2(t["ooT"], t["a3"], r)
                if step == "copy_2":
                    ac.wait_ge(t["xn3T"], r + 1)
                    nc.scalar.copy(act[:, 0, :], pb[:, 0:M])
                    nc.scalar.copy(act[0:D1, 1, :], pb[0:D1, M:2 * M]).then_inc(t["a4"], 1)
                    nc.scalar.copy(xt_[:, bass.ds(r * M, M)], pb[:, 0:M])
                    nc.scalar.copy(xtb_[0:D1, bass.ds(r * M, M)], pb[0:D1, M:2 * M]).then_inc(tokens_kept, 1)

            for n, (_, g) in enumerate(HEAD):
                square(n, n % 4, g, n < SQBUF)
                if n == LAG:
                    ac.wait_ge(columns_ready, 1)
                if n >= LAG:
                    gelu(n - LAG, (n - LAG) % 4, HEAD[n - LAG][1])
            with ac.Fori(2, NT) as i:
                for k, (_, g) in enumerate(BODY):
                    n = NHD + (i - 2) * NB + k
                    square(n, (NHD + k) % 4, g, False)
                    gelu(n - LAG, (NHD + k - LAG) % 4, BODY[k - LAG][1])
                    for step in AT[k]:
                        tokens(step, i - 2)
            def common_hidden(k):
                p, f, i = ITEMS[k]
                lo, hi = PARTS[p]
                if f is not None:
                    ac.wait_ge(c_up, UPS[k] + 1)
                    nc.scalar.activation(hc[:, f, lo * M:hi * M], ps[:, CBANK[k % 2], 0:(hi - lo) * M], ACT.Gelu)\
                        .then_inc(c_act, 1)

            for k, steps in enumerate(LAST_STEPS):
                if k < NE_SLOTS:
                    now, before = ENDING[LAG + k], ENDING[k]
                    if now is not None:
                        square(now, bank(now), ALL[now][1], False)
                    if before is not None:
                        gelu(before, bank(before), ALL[before][1])
                for step, run in steps:
                    tokens(step, run)
                if k in ITEM_AT:
                    common_hidden(ITEM_AT.index(k))

            for k in range(len(ITEM_AT), len(ITEMS)):
                common_hidden(k)
            ac.wait_ge(chosen_known, 1)
            nc.scalar.activation(lgb[:, :, :], lgb[:, :, :], ACT.Exp).then_inc(exponentials_known, 1)

            def hidden(j, b, first=False):
                ac.wait_ge(e_up, j + 1)
                if not first:
                    ac.wait_ge(e_down, j - 1)
                nc.scalar.activation(ht[:, b, :], ps[:, 2 * b:2 * b + 2, :].rearrange("p k c -> p (k c)")[:, 0:DFF],
                                     ACT.Gelu).then_inc(e_act, 1)

            hidden(0, 0, True)
            hidden(1, 1, True)
            with ac.Fori(1, (NTILE - 1) // 2) as k:
                hidden(2 * k, 0)
                hidden(2 * k + 1, 1)
            hidden(NTILE - 1, 0)


_OUTS = [((64, 12, 192), "float32")]


def kernel(**inputs):
    import numpy as _np
    import concourse.bacc as _bacc
    from concourse import mybir as _mybir
    from concourse.bass_utils import run_bass_kernel_spmd as _run

    nc = _bacc.Bacc("TRN2", target_bir_lowering=False, num_devices=1)
    arrays, args = {}, {}
    for name in inputs:
        a = _np.ascontiguousarray(inputs[name])
        arrays[f"in_{name}_dram"] = a
        args[name] = nc.dram_tensor(f"in_{name}_dram", a.shape, _mybir.dt.from_np(a.dtype), kind="ExternalInput").ap()
    outs = []
    for i, (shape, dtype) in enumerate(_OUTS):
        outs.append(nc.dram_tensor(f"out_{i}_dram", shape, _mybir.dt.from_np(_np.dtype(dtype)), kind="ExternalOutput").ap())
    audio_tower(nc, args, outs[0])
    r = _run(nc, [arrays], core_ids=[0])
    return r.results[0]["out_0_dram"]
```
